# Optimizing a Trainium2 kernel written in Bass

```python
import numpy as np
import jax
import jax.numpy as jnp

def _softmax(x, axis=-1):
    return jax.nn.softmax(x, axis=axis)

def _gelu(x):
    return jax.nn.gelu(x, approximate=True)

def _silu(x):
    return jax.nn.silu(x)

def _sigmoid(x):
    return jax.nn.sigmoid(x)

def _layernorm(x, axis=-1, eps=1e-05):
    m = jnp.mean(x, axis=axis, keepdims=True)
    v = jnp.var(x, axis=axis, keepdims=True)
    return (x - m) / jnp.sqrt(v + eps)

def _scatter_add(tgt, idx, src, axis=0):
    return tgt.at[idx].add(src)

def _segment_sum(src, seg, n):
    return jax.ops.segment_sum(src, seg, n)
kernel_name = 'mk_flamingo_gated_d1_seqx_r8_996d9e'

def setup_inputs(seed: int=0):
    np.random.seed(seed)
    _w = jnp.asarray

    def _rec_inputs():
        import jax
        import jax.numpy as jnp
        _rk = jax.random.key(seed)
        x = 7.22e-05 + 1 * jax.random.normal(jax.random.fold_in(_rk, 1), (64, 128, 128), jnp.float32)
        _lenS = 128 - jax.random.randint(jax.random.fold_in(_rk, 7), (64,), 0, max(1, 128 // 4) + 1, jnp.int32)
        _lenS2 = 120 - jax.random.randint(jax.random.fold_in(_rk, 8), (64,), 0, max(1, 120 // 4) + 1, jnp.int32)
        _ctx_768P = jax.random.normal(jax.random.fold_in(_rk, 11), (64, 16, 96), jnp.float32)
        _ctx_768c = jax.random.dirichlet(jax.random.fold_in(_rk, 511), 0.3 * jnp.ones((16,), jnp.float32), (64, 120))
        _ctx_768t = jnp.einsum('bsk,bkd->bsd', _ctx_768c, _ctx_768P)
        _ctx_768t = _ctx_768t * jax.lax.rsqrt(jnp.mean(jnp.square(_ctx_768t)) + 1e-12) * 0.953939
        ctx_768 = -0.000191848 + 0.999787 * (_ctx_768t + 0.3 * jax.random.normal(jax.random.fold_in(_rk, 611), (64, 120, 96), jnp.float32))
        _g = jax.random.normal(jax.random.fold_in(_rk, 9001), (2, 1), jnp.float32)
        _g = jnp.sign(_g) * jnp.maximum(jnp.abs(_g), 1.0) + (_g == 0) * 1.0
        g_xattn = _g[0]
        g_ffn = _g[1]
        return (x, ctx_768, g_xattn, g_ffn)
    x, ctx_768, g_xattn, g_ffn = _rec_inputs()

    def _L0_xattn_setup():
        import math
        import jax, jax.numpy as jnp
        import numpy as np
        B, SQ, SKV = (4, 256, 256)
        D_EMBED, D_CROSS, D_ATT, N_HEADS = (128, 96, 128, 16)
        D_HEAD = D_ATT // N_HEADS

        def _split_heads(t):
            b, s, _ = t.shape
            return t.reshape(b, s, N_HEADS, D_HEAD).transpose(0, 2, 1, 3)
        key = jax.random.key(seed)
        ks = jax.random.split(key, 10)
        s_e = 1.0 / math.sqrt(D_EMBED)
        s_c = 1.0 / math.sqrt(D_CROSS)
        s_a = 1.0 / math.sqrt(D_ATT)
        return {'x': jax.random.normal(ks[0], (B, SQ, D_EMBED), jnp.float32), 'y': jax.random.normal(ks[1], (B, SKV, D_CROSS), jnp.float32), 'Wq': jax.random.normal(ks[2], (D_EMBED, D_ATT), jnp.float32) * s_e, 'bq': jax.random.normal(ks[3], (D_ATT,), jnp.float32) * 0.01, 'Wk': jax.random.normal(ks[4], (D_CROSS, D_ATT), jnp.float32) * s_c, 'bk': jax.random.normal(ks[5], (D_ATT,), jnp.float32) * 0.01, 'Wv': jax.random.normal(ks[6], (D_CROSS, D_ATT), jnp.float32) * s_c, 'bv': jax.random.normal(ks[7], (D_ATT,), jnp.float32) * 0.01, 'Wo': jax.random.normal(ks[8], (D_ATT, D_EMBED), jnp.float32) * s_a, 'bo': jax.random.normal(ks[9], (D_EMBED,), jnp.float32) * 0.01}
    _L0_xattn_all = _L0_xattn_setup()
    _L0_xattn_in = {k: v for k, v in _L0_xattn_all.items() if k in ('Wq', 'bq', 'Wk', 'bk', 'Wv', 'bv', 'Wo', 'bo')}
    del _L0_xattn_all

    def _L0_ffn_setup():
        import jax, jax.numpy as jnp
        import numpy as np
        DIM = 128
        HEADS = 16
        HD = DIM // HEADS
        M = 32
        E = 4
        K = 2
        HID = 256
        MID = 256
        LB = 0.01
        EPS = 1.1920929e-07

        def _rms(x, w):
            return x * jax.lax.rsqrt(jnp.mean(x * x, axis=-1, keepdims=True) + EPS) * w

        def _gelu(x):
            return jax.nn.gelu(x, approximate=False)
        key = jax.random.key(seed)
        ks = jax.random.split(key, 20)
        d = DIM
        w = lambda k, s: jax.random.normal(k, s, jnp.float32) * 0.02
        return {'x': jax.random.normal(ks[0], (4, 128, d), jnp.float32), 'n1_w': jnp.ones((d,), jnp.float32), 'n2_w': jnp.ones((d,), jnp.float32), 'wq': w(ks[1], (d, d)), 'wk': w(ks[2], (d, d)), 'wv': w(ks[3], (d, d)), 'wo': w(ks[4], (d, d)), 'qn_w': jnp.ones((HD,), jnp.float32), 'kn_w': jnp.ones((HD,), jnp.float32), 'gate_w': w(ks[5], (E, d)), 'e0_up': w(ks[6], (HID, d)), 'e0_down': w(ks[7], (d, HID)), 'e1_w1': w(ks[8], (HID, d)), 'e1_w2': w(ks[9], (HID, d)), 'e1_down': w(ks[10], (d, HID)), 'e2_l1': w(ks[11], (MID, d)), 'e2_l2': w(ks[12], (HID, MID)), 'e2_l3': w(ks[13], (MID, HID)), 'e2_l4': w(ks[14], (d, MID)), 'e3_down': w(ks[15], (d, d)), 'e3_up': w(ks[16], (HID, d)), 'e3_out': w(ks[17], (d, HID))}
    _L0_ffn_all = _L0_ffn_setup()
    _L0_ffn_in = {k: v for k, v in _L0_ffn_all.items() if k in ('n1_w', 'n2_w', 'wq', 'wk', 'wv', 'wo', 'qn_w', 'kn_w', 'gate_w', 'e0_up', 'e0_down', 'e1_w1', 'e1_w2', 'e1_down', 'e2_l1', 'e2_l2', 'e2_l3', 'e2_l4', 'e3_down', 'e3_up', 'e3_out')}
    del _L0_ffn_all
    return {'x': x, 'ctx_768': ctx_768, 'g_xattn': g_xattn, 'g_ffn': g_ffn, 'L0_xattn_Wq': _L0_xattn_in['Wq'], 'L0_xattn_bq': _L0_xattn_in['bq'], 'L0_xattn_Wk': _L0_xattn_in['Wk'], 'L0_xattn_bk': _L0_xattn_in['bk'], 'L0_xattn_Wv': _L0_xattn_in['Wv'], 'L0_xattn_bv': _L0_xattn_in['bv'], 'L0_xattn_Wo': _L0_xattn_in['Wo'], 'L0_xattn_bo': _L0_xattn_in['bo'], 'L0_ffn_n1_w': _L0_ffn_in['n1_w'], 'L0_ffn_n2_w': _L0_ffn_in['n2_w'], 'L0_ffn_wq': _L0_ffn_in['wq'], 'L0_ffn_wk': _L0_ffn_in['wk'], 'L0_ffn_wv': _L0_ffn_in['wv'], 'L0_ffn_wo': _L0_ffn_in['wo'], 'L0_ffn_qn_w': _L0_ffn_in['qn_w'], 'L0_ffn_kn_w': _L0_ffn_in['kn_w'], 'L0_ffn_gate_w': _L0_ffn_in['gate_w'], 'L0_ffn_e0_up': _L0_ffn_in['e0_up'], 'L0_ffn_e0_down': _L0_ffn_in['e0_down'], 'L0_ffn_e1_w1': _L0_ffn_in['e1_w1'], 'L0_ffn_e1_w2': _L0_ffn_in['e1_w2'], 'L0_ffn_e1_down': _L0_ffn_in['e1_down'], 'L0_ffn_e2_l1': _L0_ffn_in['e2_l1'], 'L0_ffn_e2_l2': _L0_ffn_in['e2_l2'], 'L0_ffn_e2_l3': _L0_ffn_in['e2_l3'], 'L0_ffn_e2_l4': _L0_ffn_in['e2_l4'], 'L0_ffn_e3_down': _L0_ffn_in['e3_down'], 'L0_ffn_e3_up': _L0_ffn_in['e3_up'], 'L0_ffn_e3_out': _L0_ffn_in['e3_out']}

def reference(x, ctx_768, g_xattn, g_ffn, L0_xattn_Wq, L0_xattn_bq, L0_xattn_Wk, L0_xattn_bk, L0_xattn_Wv, L0_xattn_bv, L0_xattn_Wo, L0_xattn_bo, L0_ffn_n1_w, L0_ffn_n2_w, L0_ffn_wq, L0_ffn_wk, L0_ffn_wv, L0_ffn_wo, L0_ffn_qn_w, L0_ffn_kn_w, L0_ffn_gate_w, L0_ffn_e0_up, L0_ffn_e0_down, L0_ffn_e1_w1, L0_ffn_e1_w2, L0_ffn_e1_down, L0_ffn_e2_l1, L0_ffn_e2_l2, L0_ffn_e2_l3, L0_ffn_e2_l4, L0_ffn_e3_down, L0_ffn_e3_up, L0_ffn_e3_out):
    import jax
    import jax.numpy as jnp

    def _L0_xattn_ref(x, y, Wq, bq, Wk, bk, Wv, bv, Wo, bo):
        import math
        import jax, jax.numpy as jnp
        import numpy as np
        B, SQ, SKV = (4, 256, 256)
        D_EMBED, D_CROSS, D_ATT, N_HEADS = (128, 96, 128, 16)
        D_HEAD = D_ATT // N_HEADS

        def _split_heads(t):
            b, s, _ = t.shape
            return t.reshape(b, s, N_HEADS, D_HEAD).transpose(0, 2, 1, 3)
        q = _split_heads(x @ Wq + bq)
        k = _split_heads(y @ Wk + bk)
        v = _split_heads(y @ Wv + bv)
        scale = 1.0 / math.sqrt(D_HEAD)
        scores = jnp.einsum('bhqd,bhkd->bhqk', q, k) * scale
        weights = jax.nn.softmax(scores, axis=-1)
        out = jnp.einsum('bhqk,bhkd->bhqd', weights, v)
        out = out.transpose(0, 2, 1, 3).reshape(x.shape[0], x.shape[1], D_ATT)
        return out @ Wo + bo

    def _L0_ffn_ref(x, n1_w, n2_w, wq, wk, wv, wo, qn_w, kn_w, gate_w, e0_up, e0_down, e1_w1, e1_w2, e1_down, e2_l1, e2_l2, e2_l3, e2_l4, e3_down, e3_up, e3_out):
        import jax, jax.numpy as jnp
        import numpy as np
        DIM = 128
        HEADS = 16
        HD = DIM // HEADS
        M = 32
        E = 4
        K = 2
        HID = 256
        MID = 256
        LB = 0.01
        EPS = 1.1920929e-07

        def _rms(x, w):
            return x * jax.lax.rsqrt(jnp.mean(x * x, axis=-1, keepdims=True) + EPS) * w

        def _gelu(x):
            return jax.nn.gelu(x, approximate=False)
        B, T, C = x.shape
        h = _rms(x, n1_w)
        heads = lambda w_: (h @ w_.T).reshape(B, T, HEADS, HD).transpose(0, 2, 1, 3)
        q = _rms(heads(wq), qn_w)
        k = _rms(heads(wk), kn_w)
        v = heads(wv)
        scores = jnp.einsum('bhqd,bhkd->bhqk', q, k) * HD ** (-0.5)
        causal = jnp.tril(jnp.ones((T, T), bool))
        scores = jnp.where(causal[None, None], scores, -jnp.inf)
        attn = jax.nn.softmax(scores, axis=-1)
        ao = jnp.einsum('bhqk,bhkd->bhqd', attn, v).transpose(0, 2, 1, 3).reshape(B, T, C) @ wo.T
        ao = ao.at[:, :, :M].set(0.0)
        x = x + ao
        xf = _rms(x, n2_w).reshape(-1, C)
        N = xf.shape[0]
        logits = jnp.nan_to_num(xf @ gate_w.T)
        probs = jax.nn.softmax(logits, axis=-1)
        topv, topi = jax.lax.top_k(probs, K)
        topv = topv / (topv.sum(-1, keepdims=True) + 1e-08)
        wts = jnp.zeros((N, E), x.dtype).at[jnp.arange(N)[:, None], topi].add(topv)
        o0 = _gelu(xf @ e0_up.T) @ e0_down.T
        o1 = jax.nn.silu(xf @ e1_w1.T) * (xf @ e1_w2.T) @ e1_down.T
        o2 = _gelu(_gelu(_gelu(xf @ e2_l1.T) @ e2_l2.T) @ e2_l3.T) @ e2_l4.T
        o3 = _gelu(_gelu(xf @ e3_down.T) @ e3_up.T) @ e3_out.T
        moe = wts[:, 0:1] * o0 + wts[:, 1:2] * o1 + wts[:, 2:3] * o2 + wts[:, 3:4] * o3
        moe = moe.reshape(B, T, C).at[:, :, :M].set(0.0)
        return x + moe
    x = x + jnp.tanh(g_xattn[0]) * _L0_xattn_ref(_layernorm(x, axis=-1), ctx_768, L0_xattn_Wq, L0_xattn_bq, L0_xattn_Wk, L0_xattn_bk, L0_xattn_Wv, L0_xattn_bv, L0_xattn_Wo, L0_xattn_bo)
    x = x + jnp.tanh(g_ffn[0]) * _L0_ffn_ref(_layernorm(x, axis=-1), L0_ffn_n1_w, L0_ffn_n2_w, L0_ffn_wq, L0_ffn_wk, L0_ffn_wv, L0_ffn_wo, L0_ffn_qn_w, L0_ffn_kn_w, L0_ffn_gate_w, L0_ffn_e0_up, L0_ffn_e0_down, L0_ffn_e1_w1, L0_ffn_e1_w2, L0_ffn_e1_down, L0_ffn_e2_l1, L0_ffn_e2_l2, L0_ffn_e2_l3, L0_ffn_e2_l4, L0_ffn_e3_down, L0_ffn_e3_up, L0_ffn_e3_out)
    return x

_drawn_inputs = setup_inputs


def setup_inputs(seed=0):
    import zlib

    import numpy as np

    out = dict(_drawn_inputs(seed))
    spreads = {'L0_ffn_n1_w': (1.0, 0.2),
     'L0_ffn_n2_w': (1.0, 0.6),
     'L0_ffn_qn_w': (1.0, 0.6),
     'L0_ffn_kn_w': (1.0, 0.6)}
    factors = {'L0_xattn_bq': 8.0,
     'L0_xattn_bk': 64.0,
     'L0_xattn_bv': 6.3,
     'L0_xattn_bo': 6.232,
     'L0_ffn_e1_w1': 4.113,
     'L0_ffn_e1_w2': 4.036,
     'L0_ffn_e1_down': 4.044,
     'L0_ffn_e2_l1': 8.0,
     'L0_ffn_e2_l2': 8.0,
     'L0_ffn_e2_l3': 8.0,
     'L0_ffn_e2_l4': 8.0,
     'L0_ffn_e3_down': 8.0,
     'L0_ffn_e3_up': 8.0,
     'L0_ffn_e3_out': 8.0,
     'L0_ffn_e0_up': 8.0,
     'L0_ffn_e0_down': 8.0}
    for name, (base, spread) in spreads.items():
        noise = np.random.default_rng([zlib.crc32(name.encode()), seed]).standard_normal(out[name].shape)
        drawn = base * np.exp(spread * noise) if base else spread * noise
        out[name] = jnp.asarray(drawn.astype(out[name].dtype))
    for name, factor in factors.items():
        out[name] = (out[name] * factor).astype(out[name].dtype)
    return out
```

```python
from contextlib import ExitStack

import numpy as np

import concourse.bass as bass
from concourse import mybir

F32 = mybir.dt.float32
BF16 = mybir.dt.bfloat16
F32R = mybir.dt.float32r
ALU = mybir.AluOpType
ACT = mybir.ActivationFunctionType
AX = mybir.AxisListType

P = 128
SEQS = 64
KV = 120
DC = 96
H = 16
HD = 8
E = 4
HID = 256
KEEP = 32
UP = P - KEEP
G = 4
NG = SEQS // G
TOK = G * P
CT = G * KV
HT = 4
NT = H // HT
HALF = G // 2
VW = HD + 1
SPLIT = 3
HIGH_LOW = {"q": (0, 1, 0), "k": (0, 0, 1)}
LN_EPS = 1e-5
RMS_EPS = 1.1920929e-07
SCALE = float(HD) ** -0.5
MASKED = -1e30
F32_MAX = float(np.finfo(np.float32).max)

WCOLS = [("Wq", P), ("Wk", P), ("Wv", P), ("Wo", P), ("wqk", 2 * P), ("wv", P), ("wo", UP), ("gate", P),
         ("e0_up", HID), ("e1_w1", HID), ("e1_w2", HID), ("e2_l1", HID), ("e2_l2", 2 * HID), ("e2_l3", 2 * HID),
         ("e3_down", P), ("e3_up", HID),
         ("down0", 2 * UP), ("down1", 2 * UP), ("down2", 2 * UP), ("down3", 2 * UP)]
VCOLS = ["bq", "bk", "n1", "n2", "qn", "kn", "gx", "gf"]
ROWS = ["bv", "bo"]

M_FILLS = [("e1_w1", 0), ("e1_w2", 0), ("e1_w1", 1), ("e1_w2", 1), ("e2_l1", 0), ("e2_l1", 1), ("e0_up", 0), ("e0_up", 1),
           ("down", 1), ("e2_l2", 0), ("e2_l2", 1), ("down", 0), ("e3_down", 0), ("e2_l3", 0), ("e2_l3", 1),
           ("e3_up", 0), ("e3_up", 1), ("down", 2), ("down", 3)]
HID_AT = {"e1": 0, "e2_l1": 2, "e0_up": 4, "e2_l2": 0, "e3_down": 4, "e2_l3": 2, "e3_up": 0}
DOWN_OF = {0: "e0_up", 1: "e1", 2: "e2_l3", 3: "e3_up"}

RINGS = {"s1": ["s1a", "s1b"], "s2": ["s2a", "s2b"], "x": ["xa", "xb"], "pv": ["pv"], "t": ["t"]}
BANKS = [b for ring in RINGS.values() for b in ring]


def first_scores():
    tiles = {p: [(p, "s1", (b, c), "s1") for b in range(G) for c in range(NT)] for p in "AB"}
    fills = [("M", "fill", f, "x") for f in M_FILLS]
    between = {
        0: [("M", "squares", 0, None), ("B", "copy", 0, None)],
        1: [("M", "norm", 0, None), ("B", "norm", 0, None)],
        2: [("A", "base", 0, None), ("M", "xfT", 0, "x"), ("B", "hT", 0, "x"), ("A", "v", 0, "x")],
        3: [("M", "logits", 0, "x")],
        4: [("B", "qk", b, "x") for b in range(G)],
        5: [fills.pop(0), fills.pop(0)] + [("B", "squares", 0, None)],
        6: [fills.pop(0), fills.pop(0)] + [("B", "roots", 0, None)],
        7: [("B", "v", 0, "x"), fills.pop(0)],
        8: [("M", "gates", 0, None), fills.pop(0)],
        9: [("B", "scale", 0, None), ("B", "qT", 0, "x"), ("B", "kT", 0, "x")],
    }
    for i in range(10, len(tiles["A"])):
        between[i] = [fills.pop(0)]
    s = []
    for i, tile in enumerate(tiles["A"]):
        s += [tile] + between[i]
    s += [("A", "mT", 0, "x"), fills.pop(0)]
    left = len(fills)
    for i, tile in enumerate(tiles["B"]):
        s.append(tile)
        while fills and len(fills) > left * (len(tiles["B"]) - 3 - i) / (len(tiles["B"]) - 2):
            s.append(fills.pop(0))
    return s + fills + [("M", "store", 0, None), ("B", "mT", 0, "x")]


def second_scores():
    tiles = [(p, b, c) for half in range(G // HALF) for p in "AB" for b in range(half * HALF, (half + 1) * HALF) for c in range(NT)]
    later = {1: [("N", "load", 0, None), ("N", "norm", 0, None)], 6: [("N", "xT", 0, "x")], 9: [("N", "q", 0, "x")],
             11: [("N", "k", 0, "x")]}
    for i, (p, b, c) in enumerate(tiles):
        later.setdefault(i + 2, []).append((p, "pv", (b, c), "pv" if c == NT - 1 else None))
        if c == NT - 1:
            later.setdefault(i + 3, []).append((p, "oT", b, "t"))
            later.setdefault(i + 4, []).append((p, "nT", b, "x"))
            later.setdefault(i + 5, []).append((p, "wo", b, "x"))
            if p == "A" and b == G - 1:
                later.setdefault(i + 6, []).append(("A", "stats", 0, None))
    s = []
    for i in range(len(tiles) + 6):
        if i < len(tiles):
            p, b, c = tiles[i]
            s.append((p, "s2", (b, c), "s2"))
            if (p, b, c) == ("A", G - 1, NT - 1):
                s.append(("N", "stacks", 0, None))
        s += later.get(i, [])
    return s + [("B", "out", 0, None)]


def schedule_of_a_step():
    return first_scores() + second_scores()


SCHEDULE = schedule_of_a_step()


def bank_of_each_use():
    at, out = dict.fromkeys(RINGS, 0), {}
    for part, work, index, ring in SCHEDULE:
        if ring:
            out[part, work, index] = RINGS[ring][at[ring] % len(RINGS[ring])]
            at[ring] += 1
    return out


BANK = bank_of_each_use()


def uses_before(parts, key=None):
    n = dict.fromkeys(BANKS, 0)
    for part, work, index, ring in SCHEDULE:
        if (part, work, index) == key:
            break
        if ring and part in parts:
            n[BANK[part, work, index]] += 1
    return n


PARTS = "NABM"
RAMP = [(-1, "N"), (0, "NA"), (1, "NAB")]
LOOP = (2, NG - 1)
TAIL = [(NG - 1, "ABM"), (NG, "BM"), (NG + 1, "M")]


class Step:

    def __init__(self, t, parts):
        self.t, self.parts = t, parts
        self.works = [(p, w, i) for p, w, i, _ in SCHEDULE if p in parts]
        self.before = {k: uses_before(parts, k)[BANK[k]] for k in self.works if k in BANK}
        full = uses_before(PARTS)
        self.base = dict.fromkeys(BANKS, 0)
        for t0, p in RAMP + TAIL:
            if parts == PARTS or t0 >= t:
                continue
            for b, n in uses_before(p).items():
                self.base[b] += n
        if parts == PARTS:
            ramp = {b: sum(uses_before(p)[b] for _, p in RAMP) for b in BANKS}
            self.base = {b: t * full[b] + (ramp[b] - LOOP[0] * full[b]) for b in BANKS}
        elif t >= LOOP[1]:
            for b in BANKS:
                self.base[b] += (LOOP[1] - LOOP[0]) * full[b]

    def group(self, part):
        return self.t + 1 - PARTS.index(part)

    def first(self, part):
        return self.parts != PARTS and self.group(part) == 0

    def fills(self, *key):
        return self.base[BANK[key]] + self.before[key] + 1

    def drains(self, sources, fill=None):
        uses = {}
        for key in sources:
            uses[BANK[key]] = max(uses.get(BANK[key], 0), self.before[key] + 1)
        if fill is not None:
            uses[BANK[fill]] = max(uses.get(BANK[fill], 0), self.before[fill])
        pairs = [(bank, self.base[bank] + n) for bank, n in uses.items()]
        return [(bank, n) for bank, n in pairs if not isinstance(n, int) or n > 0]


def run_steps(engine, step):
    for t, parts in RAMP:
        step(Step(t, parts))
    with engine.Fori(*LOOP) as t:
        step(Step(t, PARTS))
    for t, parts in TAIL:
        step(Step(t, parts))


def build(nc, x, ctxT, weights, vcols, rows, out):
    ctx = ExitStack()
    with ctx:
        def sb(name, shape, dt=F32):
            return ctx.enter_context(nc.sbuf_tensor(name, shape, dt))

        def sem(name):
            return ctx.enter_context(nc.semaphore(name))

        psum = {b: ctx.enter_context(nc.psum_tensor(f"ps_{b}", [P, 512], F32)) for b in BANKS}
        filled = {b: sem(f"filled_{b}") for b in BANKS}
        drained = {b: sem(f"drained_{b}") for b in BANKS}

        W = sb("W", [P, sum(n for _, n in WCOLS)])
        at, w = 0, {}
        for name, n in WCOLS:
            w[name] = W[:, at:at + n]
            at += n
        vc = sb("vc", [P, len(VCOLS)])
        col = {n: vc[:, i:i + 1] for i, n in enumerate(VCOLS)}
        rw = sb("rw", [P, len(ROWS) * P])
        bv, bo = rw[:, 0:P], rw[:, P:2 * P]
        tg = sb("tg", [P, 2])
        gx, gf = tg[:, 0:1], tg[:, 1:2]
        qns = sb("qns", [P, 1])
        bqs = sb("bqs", [P, 1])
        gxbo = sb("gxbo", [P, P])
        identf = sb("identf", [P, P])
        identb = sb("identb", [P, P], BF16)
        neg_half = sb("neg_half", [P, G])
        rms_eps = sb("rms_eps", [P, G])
        one = sb("one", [P, 1])
        lower = sb("lower", [P, E * E])
        above = sb("above", [P, 1, P], BF16)
        pick = {"A": sb("pickA", [P, KV], BF16), "B": sb("pickB", [P, P], BF16)}

        xt, xn, x1, xy, x2, ym = (sb(n, [P, G, P]) for n in ("xt", "xn", "x1", "xy", "x2", "ym"))
        hb = xn
        ctT = sb("ctT", [DC, CT])
        xnT, xfT = (sb(n, [P, TOK]) for n in ("xnT", "xfT"))
        hT = xnT
        keys = {"A": KV, "B": P}
        whole = sb("whole", [P, TOK])
        xf = whole[:].rearrange("p (b d) -> p b d", b=G)
        split = {o: sb("split_" + o, [P, 2, TOK], F32R) for o in "qk"}
        scratch = {p + o: nc.dram_tensor(f"scratch_{p}{o}", [P * SPLIT, TOK], F32, kind="Internal").ap() for p in "AB" for o in "qk"}
        qTb = {p: sb("qTb" + p, [P, TOK], BF16) for p in "AB"}
        kTb = {p: sb("kTb" + p, [P, G * keys[p]], BF16) for p in "AB"}
        qd = {p: sb("qd" + p, [P, NT, HT, TOK], F32R) for p in "AB"}
        kst = {p: sb("kst" + p, [P, NT, G * keys[p]], F32R) for p in "AB"}
        kd = {p: sb("kd" + p, [P, H, G * keys[p]], BF16) for p in "AB"}
        mr = {p: sb("mr" + p, [P, H, HALF, P], BF16) for p in "AB"}
        V = {p: sb("V" + p, [P, G, H, VW]) for p in "AB"}
        mpad = {p: sb("mpad" + p, [P, P]) for p in "AB"}
        mneg = {p: mpad[p][:, 0:G * H].rearrange("p (a h b) -> p a h b", a=G // HALF, h=H) for p in "AB"}
        mTb = {p: sb("mTb" + p, [G * H, P], BF16) for p in "AB"}
        qk = sb("qk", [P, G, 2 * P])
        rden = sb("rden", [P, H])
        on = sb("on", [P, P])
        onT = sb("onT", [P, P])
        hid = sb("hid", [P, 6, TOK])
        sq = hid[:, 2:4].rearrange("p a (b d) -> p (a b) d", d=2 * P)
        sqM = hid[:, 2].rearrange("p (b d) -> p b d", b=G)
        probs = hid[:, 0:4]
        th, tu = hid[:, 5], hid[:, 4]
        oT = hid[:, 4]
        stA, stB = sb("stA", [P, G, 6]), sb("stB", [P, G, 6])
        mvA, mvB = sb("mvA", [P, G, 2]), sb("mvB", [P, G, 2])
        veA, veB = sb("veA", [P, G]), sb("veB", [P, G])
        rsA = sb("rsA", [P, G])
        rB = sb("rB", [P, 6, G])
        hs, hr = sb("hs", [P, 2 * H * G]), sb("hr", [P, 2 * H * G])
        ssM, msM, rM = sb("ssM", [P, G]), sb("msM", [P, G]), sb("rM", [P, G])
        lg = sb("lg", [P, 8, G, E])
        sm = sb("sm", [P, 5, G])
        cmp = sb("cmp", [P, 2, G, E, E])
        gates = sb("gates", [P, G, E])

        const_loaded = sem("const_loaded")
        setup_dve, setup_pool, setup_act = sem("setup_dve"), sem("setup_pool"), sem("setup_act")
        setup_pool_chain = sem("setup_pool_chain")
        x_loaded, ctx_loaded, stored = sem("x_loaded"), sem("ctx_loaded"), sem("stored")
        kd_loaded = {p: sem("kd_loaded" + p) for p in "AB"}
        stacks_loaded = {p: sem("stacks_loaded" + p) for p in "AB"}
        m_loaded = {p: sem("m_loaded" + p) for p in "AB"}
        cast_ready = {p: sem("cast_ready" + p) for p in "AB"}
        split_ready = {o: sem("split_ready_" + o) for o in "qk"}
        split_stored = {o: sem("split_stored_" + o) for o in "qk"}
        a_stats, a_rstd, xn_ready, x1_base = (sem(n) for n in ("a_stats", "a_rstd", "xn_ready", "x1_base"))
        x1_copied, b_stats, b_pow, b_rs, hb_ready = (sem(n) for n in ("x1_copied", "b_stats", "b_pow", "b_rs", "hb_ready"))
        sq_ready, hs_ready, root_ready, hr_ready, qk_ready = (sem(n) for n in ("sq_ready", "hs_ready", "root_ready", "hr_ready", "qk_ready"))
        y_ready = sem("y_ready")
        m_sq, m_ms, m_r, xf_ready, y_copied = (sem(n) for n in ("m_sq", "m_ms", "m_r", "xf_ready", "y_copied"))
        gate_step, gate_exp, silu_tanh = (sem(n) for n in ("gate_step", "gate_exp", "silu_tanh"))
        rden_ready = sem("rden_ready")

        GROUP_KD, GROUP_STACKS, USE_STORED = 16 * H, 16 * 2 * HT, 16 * SPLIT

        def uses_of_split(st, part):
            g = st.group(part)
            if part == "M":
                return 2 * g + 4 if not isinstance(g, int) else 2 * NG if g == NG - 1 else min(2 * g + 4, 2 * NG - 1)
            if part == "N":
                return 0 if st.first("N") else 2 * g - 1
            return min(2 * g + 2, 2 * NG - 1) if isinstance(g, int) else 2 * g + 2

        SETUP_DVE, SETUP_POOL, SETUP_ACT = 1, 1, 1
        GATE_STEPS = 16
        block = ctx.enter_context(nc.Block())

        @block.sync
        def _(sp):
            sp.dma_start(W[:], weights).then_inc(const_loaded, 16)
            sp.dma_start(vc[:], vcols).then_inc(const_loaded, 16)
            sp.dma_start(rw[:], rows).then_inc(const_loaded, 16)

            def store_split(st, part, to, o):
                n, g = uses_of_split(st, part), st.group(part)
                if not st.first(part):
                    sp.wait_ge(stacks_loaded[to], g * GROUP_STACKS)
                sp.wait_ge(split_ready[o], n * 2 + 2)
                width = G * keys[to] if o == "k" else TOK
                rows3 = scratch[to + o].rearrange("(p s) t -> p s t", s=SPLIT)
                for s in range(SPLIT):
                    sp.dma_start(rows3[:, s, 0:width], split[o][:, HIGH_LOW[o][s], 0:width].bitcast(F32)).then_inc(split_stored[o], 16)

            def load_stacks(st, part, to):
                n = uses_of_split(st, part)
                sp.wait_ge(split_stored["q"], n * USE_STORED + USE_STORED)
                sp.wait_ge(split_stored["k"], n * USE_STORED + USE_STORED)
                rows = HD * SPLIT
                for j in range(HT):
                    at = slice(32 * j, 32 * j + rows)
                    q, k = (scratch[to + o].rearrange("(c j r) t -> j r c t", j=HT, r=rows)[j] for o in "qk")
                    sp.dma_start(qd[to][at, :, j, :].bitcast(F32), q).then_inc(stacks_loaded[to], 16)
                    sp.dma_start(kst[to][at, :, :].bitcast(F32), k[:, :, 0:G * keys[to]]).then_inc(stacks_loaded[to], 16)

            def load_block_diagonal_keys(st, part, to):
                sp.wait_ge(cast_ready[to], st.group(part) * 2 + 2)
                for h in range(H):
                    r = slice(h * HD, h * HD + HD)
                    sp.dma_start(kd[to][r, h, :], kTb[to][r, :]).then_inc(kd_loaded[to], 16)

            def step(st):
                for part, work, index in st.works:
                    g = st.group(part)
                    if (part, work) == ("N", "load"):
                        if not st.first("N"):
                            sp.wait_ge(xn_ready, g)
                            sp.wait_ge(x1_base, g)
                            sp.wait_ge(filled[BANK["A", "v", 0]], st.fills("A", "v", 0))
                        sp.dma_start(xt[:], x[bass.ds(g * G, G), :, :].rearrange("b t d -> t b d")).then_inc(x_loaded, 16)
                        sp.dma_start(ctT[:], ctxT[:, bass.ds(g * CT, CT)]).then_inc(ctx_loaded, 16)
                    elif (part, work) == ("N", "k"):
                        load_block_diagonal_keys(st, "N", "A")
                        store_split(st, "N", "A", "q")
                        store_split(st, "N", "A", "k")
                        if st.parts == "N":
                            load_stacks(st, "N", "A")
                    elif (part, work) == ("N", "stacks") and st.parts != "N":
                        sp.wait_ge(filled[BANK["A", "s2", (G - 1, NT - 1)]], st.fills("A", "s2", (G - 1, NT - 1)))
                        load_stacks(st, "N", "A")
                    elif (part, work) == ("B", "kT"):
                        load_block_diagonal_keys(st, "B", "B")
                        store_split(st, "B", "B", "q")
                        store_split(st, "B", "B", "k")
                        load_stacks(st, "B", "B")
                    elif work == "mT":
                        sp.wait_ge(drained[BANK[part, "mT", 0]], st.fills(part, "mT", 0))
                        sp.dma_start(mr[part][P - 1:P, :, :, :].rearrange("p h b q -> p (h b) q"),
                                     mTb[part][0:H * HALF, :]).then_inc(m_loaded[part], 16)
                    elif work == "s2" and index == (HALF - 1, NT - 1):
                        sp.wait_ge(filled[BANK[part, work, index]], st.fills(part, work, index))
                        sp.dma_start(mr[part][P - 1:P, :, :, :].rearrange("p h b q -> p (h b) q"),
                                     mTb[part][H * HALF:2 * H * HALF, :]).then_inc(m_loaded[part], 16)

            sp.wait_ge(setup_pool, SETUP_POOL)
            sp.wait_ge(setup_dve, SETUP_DVE)
            run_steps(sp, step)

        @block.gpsimd
        def _(pool):
            chain = [0]

            def link(ins):
                chain[0] += 1
                ins.then_inc(setup_pool_chain, 1)
                pool.wait_ge(setup_pool_chain, chain[0])

            link(pool.memset(identf[:], 0.0))
            link(pool.affine_select(out=identf[:], in_=identf[:], compare_op=ALU.not_equal, fill=1.0, base=0,
                                    pattern=[[-1, P]], channel_multiplier=1))
            link(pool.tensor_copy(identb[:], identf[:]))
            link(pool.memset(above[:], 0.0))
            link(pool.affine_select(out=above[:], in_=above[:], compare_op=ALU.is_ge, fill=MASKED, base=0,
                                    pattern=[[0, 1], [-1, P]], channel_multiplier=1))
            link(pool.tensor_copy(pick["B"][:], above[:, 0, :]))
            link(pool.affine_select(out=pick["B"][:], in_=pick["B"][:], compare_op=ALU.is_ge, fill=1.0,
                                    base=P - 2, pattern=[[0, P]], channel_multiplier=-1))
            link(pool.memset(pick["A"][:], 0.0))
            link(pool.affine_select(out=pick["A"][:], in_=pick["A"][:], compare_op=ALU.is_ge, fill=1.0,
                                    base=P - 2, pattern=[[0, KV]], channel_multiplier=-1))
            link(pool.memset(mr["A"][:], 0.0))
            link(pool.memset(mr["B"][:], 0.0))
            link(pool.affine_select(out=mr["B"][:].rearrange("p h b q -> p (h b) q"),
                                    in_=mr["B"][:].rearrange("p h b q -> p (h b) q"), compare_op=ALU.not_equal,
                                    fill=1.0, base=0, pattern=[[0, H * HALF], [-1, P]], channel_multiplier=1))
            link(pool.memset(neg_half[:], -0.5))
            link(pool.memset(rms_eps[:], RMS_EPS))
            link(pool.memset(one[:], 1.0))
            link(pool.memset(lower[:], 0.0))
            for e in range(E):
                if e:
                    link(pool.memset(lower[:, e * E:e * E + e], 1.0))
            pool.wait_ge(setup_act, SETUP_ACT)
            link(pool.tensor_tensor(gxbo[:], bo, gx.to_broadcast([P, P]), ALU.mult))
            pool.memset(V["A"][:, :, :, HD:VW], 1.0)
            link(pool.memset(V["B"][:, :, :, HD:VW], 1.0))
            pool.memset(rB[:], 0.0).then_inc(setup_pool, 1)
            pool.wait_ge(setup_pool, 1)
            ones = one[:].rearrange("p (a b) -> p a b", a=1).to_broadcast([P, G, P])

            def step(st):
                for part, work, index in st.works:
                    g = st.group(part)
                    if (part, work) == ("N", "norm"):
                        pool.wait_ge(a_stats, g * 3 + 3)
                        pool.tensor_tensor(rsA[:], veA[:], neg_half[:], ALU.pow).then_inc(a_rstd, 1)
                    elif (part, work) == ("M", "squares"):
                        pool.wait_ge(y_ready, g + 1)
                        pool.tensor_tensor(sqM, x2[:], x2[:], ALU.mult).then_inc(m_sq, 1)
                        if not st.first("M"):
                            pool.wait_ge(stored, g * 16)
                        pool.tensor_tensor(ym[:], xy[:], ones, ALU.mult).then_inc(y_copied, 1)
                    elif (part, work) == ("M", "norm"):
                        pool.wait_ge(m_ms, g * 2 + 2)
                        pool.tensor_tensor(rM[:], msM[:], neg_half[:], ALU.pow).then_inc(m_r, 1)
                    elif (part, work) == ("B", "copy"):
                        pool.wait_ge(b_stats, g * 3 + 3)
                        if not st.first("B"):
                            pool.wait_ge(y_copied, g)
                        pool.tensor_tensor(xy[:], x1[:], ones, ALU.mult).then_inc(x1_copied, 1)
                    elif (part, work) == ("A", "stats"):
                        pool.wait_ge(b_stats, g * 3 + 3)
                        pool.tensor_tensor(rB[:, 0], veB[:], neg_half[:], ALU.pow).then_inc(b_pow, 1)
                        pool.wait_ge(b_pow, g * 5 + 1)
                        pool.tensor_tensor(rB[:, 1], rB[:, 0], rB[:, 0], ALU.mult).then_inc(b_pow, 1)
                        pool.wait_ge(b_pow, g * 5 + 2)
                        pool.tensor_tensor(rB[:, 2], rB[:, 1], mvB[:, :, 1], ALU.mult).then_inc(b_pow, 1)
                        pool.wait_ge(b_pow, g * 5 + 3)
                        pool.tensor_tensor(rB[:, 3], rB[:, 2], rms_eps[:], ALU.add).then_inc(b_pow, 1)
                        pool.wait_ge(b_pow, g * 5 + 4)
                        pool.tensor_tensor(rB[:, 4], rB[:, 3], neg_half[:], ALU.pow).then_inc(b_pow, 1)
                        pool.wait_ge(b_pow, g * 5 + 5)
                        pool.tensor_tensor(rB[:, 5], rB[:, 4], rB[:, 0], ALU.mult).then_inc(b_rs, 1)
                    elif (part, work) == ("A", "base"):
                        if not st.first("A"):
                            pool.wait_ge(hb_ready, g)
                            pool.wait_ge(x1_copied, g)
                        pool.wait_ge(x_loaded, g * 16 + 16)
                        pool.tensor_tensor(x1[:], xt[:], gxbo[:].rearrange("p (a d) -> p a d", a=1).to_broadcast([P, G, P]),
                                           ALU.add).then_inc(x1_base, 1)
                    elif (part, work) == ("B", "squares"):
                        for bank, n in st.drains([("B", "qk", b) for b in range(G)]):
                            pool.wait_ge(drained[bank], n)
                        if not st.first("B"):
                            pool.wait_ge(m_ms, g * 2 - 1)
                        pool.tensor_tensor(sq, qk[:], qk[:], ALU.mult).then_inc(sq_ready, 1)
                    elif (part, work) == ("M", "store"):
                        for bank, n in st.drains([("M", "fill", ("down", e)) for e in range(E)]):
                            pool.wait_ge(drained[bank], n)
                        pool.dma_start(out[bass.ds(g * G, G), :, :].rearrange("b t d -> t b d"), ym[:]).then_inc(stored, 16)

            run_steps(pool, step)
            pool.wait_ge(stored, NG * 16)

        @block.scalar
        def _(act):
            act.wait_ge(const_loaded, 48)
            nc.scalar.activation(tg[:], vc[:, len(VCOLS) - 2:len(VCOLS)], ACT.Tanh).then_inc(setup_act, 1)
            act.wait_ge(setup_dve, SETUP_DVE)

            def queries_or_keys(st, part, to, o, **affine):
                key = (part, {"N": o, "B": o + "T"}[part], 0)
                width = G * keys[to] if o == "k" else TOK
                bank = psum[BANK[key]][:, 0:width]
                act.wait_ge(filled[BANK[key]], st.fills(*key))
                nc.scalar.activation((qTb if o == "q" else kTb)[to][:], bank, ACT.Identity, **affine).then_inc(cast_ready[to], 1)
                n = uses_of_split(st, part)
                if o == "k":
                    act.wait_ge(split_ready["q"], n * 2 + 2)
                elif not isinstance(n, int) or n > 0:
                    act.wait_ge(split_ready["k"], n * 2)
                nc.scalar.activation(whole[:, 0:width], bank, ACT.Identity, **affine).then_inc(drained[BANK[key]], 1)

            def step(st):
                for part, work, index in st.works:
                    key, g = (part, work, index), st.group(part)
                    if key in BANK:
                        bank, full, done = psum[BANK[key]], filled[BANK[key]], drained[BANK[key]]
                    if (part, work) == ("N", "xT"):
                        act.wait_ge(full, st.fills(*key))
                        nc.scalar.activation(xnT[:], bank[:], ACT.Copy).then_inc(done, 1)
                    elif (part, work) == ("N", "q"):
                        queries_or_keys(st, "N", "A", "q", bias=bqs[:], scale=SCALE)
                    elif (part, work) == ("N", "k"):
                        queries_or_keys(st, "N", "A", "k", bias=col["bk"])
                    elif (part, work) == ("M", "xfT"):
                        act.wait_ge(full, st.fills(*key))
                        nc.scalar.activation(xfT[:], bank[:], ACT.Identity, scale=col["n2"]).then_inc(done, 1)
                    elif (part, work) == ("B", "hT"):
                        act.wait_ge(full, st.fills(*key))
                        nc.scalar.activation(hT[:], bank[:], ACT.Identity, scale=col["n1"]).then_inc(done, 1)
                    elif (part, work) == ("B", "qk"):
                        act.wait_ge(full, st.fills(*key))
                        nc.scalar.activation(qk[:, index, :], bank[:, 0:2 * P], ACT.Copy).then_inc(done, 1)
                    elif (part, work) == ("B", "v"):
                        act.wait_ge(full, st.fills(*key))
                        nc.scalar.activation(V["B"][:, :, :, 0:HD].rearrange("p b h d -> p (b h) d"),
                                             bank[:].rearrange("p (n d) -> p n d", d=HD), ACT.Copy).then_inc(done, 1)
                    elif (part, work) == ("B", "roots"):
                        act.wait_ge(hs_ready, g * 2 + 2)
                        nc.scalar.activation(hr[:], hs[:], ACT.Sqrt).then_inc(root_ready, 1)
                    elif (part, work) == ("B", "qT"):
                        queries_or_keys(st, "B", "B", "q", scale=qns[:])
                    elif (part, work) == ("B", "kT"):
                        queries_or_keys(st, "B", "B", "k", scale=col["kn"])
                    elif (part, work) == ("M", "gates"):
                        act.wait_ge(gate_step, g * GATE_STEPS + 3)
                        nc.scalar.activation(lg[:, 3], lg[:, 2], ACT.Exp).then_inc(gate_exp, 1)
                    elif work == "mT":
                        act.wait_ge(full, st.fills(*key))
                        nc.scalar.activation(mTb[part][:], bank[0:G * H, 0:P], ACT.Copy).then_inc(done, 1)
                    elif work == "fill" and index[0] == "e1_w1":
                        if index[1]:
                            for b, n in st.drains([("M", "fill", ("e1_w1", index[1] - 1))]):
                                act.wait_ge(drained[b], n)
                        act.wait_ge(full, st.fills(*key))
                        nc.scalar.activation(th, bank[:], ACT.Tanh, scale=0.5).then_inc(silu_tanh, 1)
                    elif work == "fill" and index[0] in HID_AT:
                        if index == ("e0_up", 0):
                            for b, n in st.drains([("M", "fill", ("e1_w1", 1)), ("M", "fill", ("e1_w2", 1))]):
                                act.wait_ge(drained[b], n)
                        act.wait_ge(full, st.fills(*key))
                        nc.scalar.activation(hid[:, HID_AT[index[0]] + index[1], :], bank[:], ACT.Gelu).then_inc(done, 1)
                    elif work == "s2":
                        k = keys[part]
                        act.wait_ge(full, st.fills(*key))
                        nc.scalar.activation(probs[0:k, index[1], :], bank[0:k, :], ACT.Exp).then_inc(done, 1)
                    elif work == "pv" and index[1] == NT - 1:
                        act.wait_ge(full, st.fills(*key))
                        nc.scalar.activation(oT, bank[:], ACT.Copy).then_inc(done, 1)
                    elif work == "nT":
                        act.wait_ge(full, st.fills(*key))
                        nc.scalar.activation(onT[:], bank[:, 0:P], ACT.Copy).then_inc(done, 1)

            run_steps(act, step)

        @block.vector
        def _(dve):
            def statistics(src, stats_of, mv, ve, stats, g):
                for b in range(G):
                    ins = nc.vector.bn_stats(stats_of[:, b, :], src[:, b, :])
                ins.then_inc(stats, 1)
                dve.wait_ge(stats, g * 3 + 1)
                nc.vector.memset(sm[:, 4, 3:4], 0.0)
                for b in range(G):
                    ins = nc.vector.bn_aggr(mv[:, b, :], stats_of[:, b, :])
                ins.then_inc(stats, 1)
                dve.wait_ge(stats, g * 3 + 2)
                nc.vector.tensor_scalar(ve[:], mv[:, :, 1], LN_EPS, None, ALU.add).then_inc(stats, 1)

            def split_rows(st, part, to, o):
                key = (part, {"N": o, "B": o + "T"}[part], 0)
                width = G * keys[to] if o == "k" else TOK
                n = uses_of_split(st, part)
                if not isinstance(n, int) or n > 0:
                    dve.wait_ge(split_stored[o], n * USE_STORED)
                dve.wait_ge(drained[BANK[key]], st.fills(*key))
                nc.vector.tensor_copy(split[o][:, 0, 0:width], whole[:, 0:width]).then_inc(split_ready[o], 1)
                dve.wait_ge(split_ready[o], n * 2 + 1)
                nc.vector.tensor_tensor(split[o][:, 1, 0:width], whole[:, 0:width], split[o][:, 0, 0:width].bitcast(F32),
                                        ALU.subtract).then_inc(split_ready[o], 1)

            def step(st):
                for part, work, index in st.works:
                    key, g = (part, work, index), st.group(part)
                    if key in BANK:
                        bank, full, done = psum[BANK[key]], filled[BANK[key]], drained[BANK[key]]
                    if (part, work) == ("N", "norm"):
                        dve.wait_ge(x_loaded, g * 16 + 16)
                        statistics(xt, stA, mvA, veA, a_stats, g)
                        dve.wait_ge(a_rstd, g + 1)
                        for b in range(G):
                            ins = nc.vector.tensor_scalar(xn[:, b, :], xt[:, b, :], mvA[:, b, 0:1], rsA[:, b:b + 1],
                                                          ALU.subtract, ALU.mult)
                        ins.then_inc(xn_ready, 1)
                    elif (part, work) == ("A", "stats"):
                        for b, n in st.drains([("A", "wo", b) for b in range(G)]):
                            dve.wait_ge(drained[b], n)
                        statistics(x1, stB, mvB, veB, b_stats, g)
                    elif (part, work) == ("B", "norm"):
                        if not st.first("B"):
                            dve.wait_ge(xf_ready, g)
                        dve.wait_ge(b_rs, g + 1)
                        for b in range(G):
                            nc.vector.tensor_scalar(x2[:, b, :], x1[:, b, :], mvB[:, b, 0:1], rB[:, 0, b:b + 1],
                                                    ALU.subtract, ALU.mult)
                            ins = nc.vector.tensor_scalar(hb[:, b, :], x1[:, b, :], mvB[:, b, 0:1], rB[:, 5, b:b + 1],
                                                          ALU.subtract, ALU.mult)
                        ins.then_inc(hb_ready, 1)
                    elif (part, work) == ("M", "squares"):
                        dve.wait_ge(m_sq, g + 1)
                        nc.vector.tensor_reduce(ssM[:], sqM, AX.X, ALU.add).then_inc(m_ms, 1)
                        dve.wait_ge(m_ms, g * 2 + 1)
                        nc.vector.tensor_scalar(msM[:], ssM[:], 1.0 / P, RMS_EPS, ALU.mult, ALU.add).then_inc(m_ms, 1)
                    elif (part, work) == ("M", "norm"):
                        dve.wait_ge(split_ready["k"], uses_of_split(st, "M") * 2)
                        dve.wait_ge(m_r, g + 1)
                        for b in range(G):
                            ins = nc.vector.tensor_scalar(xf[:, b, :], x2[:, b, :], rM[:, b:b + 1], None, ALU.mult)
                        ins.then_inc(xf_ready, 1)
                    elif (part, work) in (("N", "q"), ("N", "k")):
                        split_rows(st, "N", "A", work)
                    elif (part, work) in (("B", "qT"), ("B", "kT")):
                        split_rows(st, "B", "B", work[0])
                    elif (part, work) == ("A", "v"):
                        dve.wait_ge(full, st.fills(*key))
                        for b in range(G):
                            ins = nc.vector.tensor_tensor(
                                V["A"][0:KV, b, :, 0:HD], bank[0:KV, b * P:(b + 1) * P].rearrange("p (h d) -> p h d", h=H),
                                bv[0:KV, :].rearrange("p (h d) -> p h d", h=H), ALU.add)
                        ins.then_inc(done, 1)
                    elif (part, work) == ("B", "roots"):
                        dve.wait_ge(sq_ready, g + 1)
                        nc.vector.tensor_reduce(hs[:], sq.rearrange("p b (h d) -> p (b h) d", d=HD), AX.X, ALU.add)\
                            .then_inc(hs_ready, 1)
                        dve.wait_ge(hs_ready, g * 2 + 1)
                        nc.vector.tensor_scalar(hs[:], hs[:], 1.0 / HD, RMS_EPS, ALU.mult, ALU.add).then_inc(hs_ready, 1)
                    elif (part, work) == ("B", "scale"):
                        dve.wait_ge(root_ready, g + 1)
                        nc.vector.reciprocal(hr[:], hr[:]).then_inc(hr_ready, 1)
                        dve.wait_ge(hr_ready, g + 1)
                        nc.vector.tensor_tensor(
                            qk[:].rearrange("p b (h d) -> p (b h) d", d=HD), qk[:].rearrange("p b (h d) -> p (b h) d", d=HD),
                            hr[:].rearrange("p (n a) -> p n a", a=1).to_broadcast([P, 2 * H * G, HD]), ALU.mult)\
                            .then_inc(qk_ready, 1)
                    elif (part, work) == ("M", "logits"):
                        logits = bank[:].rearrange("p (b e) -> p b e", b=G)[:, :, 0:E]
                        dve.wait_ge(full, st.fills(*key))
                        nc.vector.tensor_scalar(lg[:, 0], logits, 0.0, F32_MAX, ALU.max, ALU.min)
                        nc.vector.tensor_scalar(lg[:, 1], logits, 0.0, -F32_MAX, ALU.min, ALU.max).then_inc(done, 1)
                    elif (part, work) == ("M", "gates"):
                        choose_experts(st, g)
                    elif work == "s1":
                        b, c = index
                        k = keys[part]
                        dve.wait_ge(full, st.fills(*key))
                        nc.vector.tensor_reduce(mneg[part][:, b // HALF, c * HT:(c + 1) * HT, b % HALF],
                                                bank[:, 0:HT * k].rearrange("p (h k) -> p h k", h=HT),
                                                AX.X, ALU.max, negate=True).then_inc(done, 1)
                    elif work == "fill" and index[0] == "e1_w2":
                        c = index[1]
                        u = BANK["M", "fill", ("e1_w1", c)]
                        if c:
                            for b, n in st.drains([("M", "fill", ("e1_w2", c - 1))]):
                                dve.wait_ge(drained[b], n)
                        dve.wait_ge(silu_tanh, g * 2 + c + 1)
                        nc.vector.scalar_tensor_tensor(out=tu, in0=th, scalar=1.0, in1=psum[u][:],
                                                       op0=ALU.add, op1=ALU.mult).then_inc(drained[u], 1)
                        dve.wait_ge(drained[u], st.fills("M", "fill", ("e1_w1", c)))
                        dve.wait_ge(full, st.fills(*key))
                        nc.vector.scalar_tensor_tensor(out=hid[:, HID_AT["e1"] + c, :], in0=tu, scalar=0.5, in1=bank[:],
                                                       op0=ALU.mult, op1=ALU.mult).then_inc(done, 1)
                    elif work == "fill" and index[0] == "down":
                        e = index[1]
                        order = [f for f in M_FILLS if f[0] == "down"]
                        n = order.index(index)
                        if n == 0:
                            dve.wait_ge(y_copied, g + 1)
                        else:
                            for b, v in st.drains([("M", "fill", order[n - 1])]):
                                dve.wait_ge(drained[b], v)
                        dve.wait_ge(full, st.fills(*key))
                        for b in range(G):
                            ins = nc.vector.scalar_tensor_tensor(
                                out=ym[:, b, KEEP:P], in0=bank[:, b * UP:(b + 1) * UP], scalar=gates[:, b, e:e + 1],
                                in1=ym[:, b, KEEP:P], op0=ALU.mult, op1=ALU.add)
                        ins.then_inc(done, 1)
                    elif work == "oT":
                        dve.wait_ge(full, st.fills(*key))
                        v = bank[:].rearrange("p (h e) -> p h e", h=H)
                        nc.vector.reciprocal(rden[:].rearrange("p (h a) -> p h a", a=1), v[:, :, HD:VW]).then_inc(rden_ready, 1)
                        dve.wait_ge(rden_ready, st.fills(*key))
                        nc.vector.tensor_tensor(on[:].rearrange("p (h d) -> p h d", h=H), v[:, :, 0:HD],
                                                rden[:].rearrange("p (h a) -> p h a", a=1).to_broadcast([P, H, HD]),
                                                ALU.mult).then_inc(done, 1)
                    elif work == "wo" and part == "A":
                        if index == 0:
                            dve.wait_ge(x1_base, g + 1)
                        dve.wait_ge(full, st.fills(*key))
                        nc.vector.scalar_tensor_tensor(out=x1[:, index, :], in0=bank[:, 0:P], scalar=gx, in1=x1[:, index, :],
                                                       op0=ALU.mult, op1=ALU.add).then_inc(done, 1)
                    elif work == "wo":
                        dve.wait_ge(full, st.fills(*key))
                        nc.vector.tensor_tensor(x2[:, index, KEEP:P], bank[:, 0:UP], x2[:, index, KEEP:P],
                                                ALU.add).then_inc(done, 1)
                    elif (part, work) == ("B", "out"):
                        for b, n in st.drains([("B", "wo", b) for b in range(G)]):
                            dve.wait_ge(drained[b], n)
                        dve.wait_ge(x1_copied, g + 1)
                        nc.vector.scalar_tensor_tensor(out=xy[:], in0=x2[:], scalar=gf, in1=xy[:],
                                                       op0=ALU.mult, op1=ALU.add).then_inc(y_ready, 1)

            def choose_experts(st, g):
                spot = BANK["M", "logits", 0]
                n = [0]

                def link(ins):
                    ins.then_inc(gate_step, 1)
                    n[0] += 1
                    dve.wait_ge(gate_step, g * GATE_STEPS + n[0])

                def over_experts(a):
                    return a.rearrange("p (b a) -> p b a", a=1).to_broadcast([P, G, E])

                dve.wait_ge(drained[spot], st.fills("M", "logits", 0))
                link(nc.vector.tensor_tensor(lg[:, 4], lg[:, 0], lg[:, 1], ALU.add))
                link(nc.vector.tensor_reduce(sm[:, 0], lg[:, 4], AX.X, ALU.max, negate=True))
                link(nc.vector.tensor_tensor(lg[:, 2], lg[:, 4], over_experts(sm[:, 0]), ALU.add))
                dve.wait_ge(gate_exp, g + 1)
                link(nc.vector.tensor_reduce(sm[:, 1], lg[:, 3], AX.X, ALU.add))
                link(nc.vector.reciprocal(sm[:, 2], sm[:, 1]))
                link(nc.vector.tensor_tensor(lg[:, 5], lg[:, 3], over_experts(sm[:, 2]), ALU.mult))
                p_j = lg[:, 5].rearrange("p b (a e) -> p b a e", a=1).to_broadcast([P, G, E, E])
                p_e = lg[:, 5].rearrange("p b (e a) -> p b e a", a=1).to_broadcast([P, G, E, E])
                for b in range(G):
                    pj, pe_ = p_j[:, b], p_e[:, b]
                    nc.vector.tensor_tensor(cmp[:, 0, b], pj, pe_, ALU.is_gt)
                    last = nc.vector.tensor_tensor(cmp[:, 1, b], pj, pe_, ALU.is_equal)
                link(last)
                link(nc.vector.tensor_tensor(cmp[:, 1].rearrange("p b e j -> p b (e j)"), cmp[:, 1].rearrange("p b e j -> p b (e j)"),
                                             lower[:].rearrange("p (a n) -> p a n", a=1).to_broadcast([P, G, E * E]), ALU.mult))
                link(nc.vector.tensor_tensor(cmp[:, 0].rearrange("p b e j -> p (b e j)"), cmp[:, 0].rearrange("p b e j -> p (b e j)"),
                                             cmp[:, 1].rearrange("p b e j -> p (b e j)"), ALU.add))
                link(nc.vector.tensor_reduce(lg[:, 6], cmp[:, 0], AX.X, ALU.add))
                link(nc.vector.tensor_scalar(lg[:, 7], lg[:, 6], 1.5, None, ALU.is_lt))
                link(nc.vector.tensor_tensor(lg[:, 6], lg[:, 5], lg[:, 7], ALU.mult))
                link(nc.vector.tensor_reduce(sm[:, 3], lg[:, 6], AX.X, ALU.add))
                link(nc.vector.tensor_scalar(sm[:, 1], sm[:, 3], 1e-8, None, ALU.add))
                link(nc.vector.reciprocal(sm[:, 2], sm[:, 1]))
                link(nc.vector.scalar_tensor_tensor(out=gates[:], in0=lg[:, 6], scalar=gf, in1=over_experts(sm[:, 2]),
                                                    op0=ALU.mult, op1=ALU.mult))
                assert n[0] == GATE_STEPS

            for p in "AB":
                nc.vector.memset(qd[p][:].bitcast(F32), 0.0)
                nc.vector.memset(kst[p][:].bitcast(F32), 0.0)
                nc.vector.memset(kd[p][:], 0.0)
                nc.vector.memset(mpad[p][:], 0.0)
            nc.vector.memset(psum["pv"][:], 0.0)
            dve.wait_ge(const_loaded, 48)
            dve.wait_ge(setup_act, SETUP_ACT)
            dve.wait_ge(setup_pool, SETUP_POOL)
            nc.vector.tensor_scalar(bqs[:], col["bq"], SCALE, None, ALU.mult)
            nc.vector.tensor_scalar(qns[:], col["qn"], SCALE, None, ALU.mult).then_inc(setup_dve, 1)
            dve.wait_ge(setup_dve, 1)
            run_steps(dve, step)

        @block.tensor
        def _(pe):
            pe.wait_ge(setup_dve, SETUP_DVE)
            mm = nc.tensor.matmul

            def transposes(st, key, of, n, sources=()):
                for b, v in st.drains(sources, key):
                    pe.wait_ge(drained[b], v)
                for b in range(n):
                    ins = nc.tensor.transpose(psum[BANK[key]][:, b * P:(b + 1) * P], of(b), identf[:])
                ins.then_inc(filled[BANK[key]], 1)

            def step(st):
                for part, work, index in st.works:
                    key, g = (part, work, index), st.group(part)
                    if key in BANK:
                        bank, done = psum[BANK[key]], filled[BANK[key]]
                    if (part, work) == ("N", "xT"):
                        pe.wait_ge(xn_ready, g + 1)
                        transposes(st, key, lambda b: xn[:, b, :], G)
                    elif (part, work) == ("N", "q"):
                        for b, v in st.drains([("N", "xT", 0)], key):
                            pe.wait_ge(drained[b], v)
                        mm(bank[:], w["Wq"], xnT[:], start=True, stop=True).then_inc(done, 1)
                    elif (part, work) == ("N", "k"):
                        pe.wait_ge(ctx_loaded, g * 16 + 16)
                        for b, v in st.drains([], key):
                            pe.wait_ge(drained[b], v)
                        mm(bank[:, 0:CT], w["Wk"][0:DC, :], ctT[:], start=True, stop=True).then_inc(done, 1)
                    elif (part, work) == ("A", "v"):
                        for b, v in st.drains([], key):
                            pe.wait_ge(drained[b], v)
                        for b in range(G):
                            ins = mm(bank[0:KV, b * P:(b + 1) * P], ctT[:, b * KV:(b + 1) * KV], w["Wv"][0:DC, :],
                                     start=True, stop=True)
                        ins.then_inc(done, 1)
                    elif (part, work) == ("M", "xfT"):
                        pe.wait_ge(xf_ready, g + 1)
                        transposes(st, key, lambda b: xf[:, b, :], G)
                    elif (part, work) == ("M", "logits"):
                        for b, v in st.drains([("M", "xfT", 0)], key):
                            pe.wait_ge(drained[b], v)
                        for b in range(G):
                            ins = mm(bank[:, b * P:(b + 1) * P], xfT[:, b * P:(b + 1) * P], w["gate"], start=True, stop=True)
                        ins.then_inc(done, 1)
                    elif (part, work) == ("B", "hT"):
                        pe.wait_ge(hb_ready, g + 1)
                        transposes(st, key, lambda b: hb[:, b, :], G)
                    elif (part, work) == ("B", "qk"):
                        for b, v in st.drains([("B", "hT", 0)], key):
                            pe.wait_ge(drained[b], v)
                        mm(bank[:, 0:2 * P], hT[:, index * P:(index + 1) * P], w["wqk"], start=True, stop=True).then_inc(done, 1)
                    elif (part, work) == ("B", "v"):
                        for b, v in st.drains([], key):
                            pe.wait_ge(drained[b], v)
                        for b in range(G):
                            ins = mm(bank[:, b * P:(b + 1) * P], hT[:, b * P:(b + 1) * P], w["wv"], start=True, stop=True)
                        ins.then_inc(done, 1)
                    elif (part, work) in (("B", "qT"), ("B", "kT")):
                        pe.wait_ge(qk_ready, g + 1)
                        first = 0 if work == "qT" else P
                        transposes(st, key, lambda b: qk[:, b, first:first + P], G)
                    elif work == "s1":
                        b, c = index
                        k = keys[part]
                        if index == (0, 0):
                            pe.wait_ge(cast_ready[part], g * 2 + 2)
                            pe.wait_ge(kd_loaded[part], g * GROUP_KD + GROUP_KD)
                        for bk, v in st.drains([], key):
                            pe.wait_ge(drained[bk], v)
                        o = bank[:, 0:HT * k].rearrange("p (h k) -> p h k", h=HT)
                        ins = mm(o, qTb[part][:, b * P:(b + 1) * P], kd[part][:, c * HT:(c + 1) * HT, b * k:(b + 1) * k],
                                 start=True, stop=part == "A")
                        if part == "B":
                            ins = mm(o, identb[:], above[:].to_broadcast([P, HT, P]), start=False, stop=True)
                        ins.then_inc(done, 1)
                    elif work == "mT":
                        for b, v in st.drains([(part, "s1", (G - 1, NT - 1)), (part, "s1", (G - 1, NT - 2))], key):
                            pe.wait_ge(drained[b], v)
                        nc.tensor.transpose(bank[:, 0:P], mpad[part][:], identf[:]).then_inc(done, 1)
                    elif work == "s2":
                        b, c = index
                        k = keys[part]
                        if index == (0, 0):
                            pe.wait_ge(stacks_loaded[part], g * GROUP_STACKS + GROUP_STACKS)
                        if b % HALF == 0 and c == 0:
                            pe.wait_ge(m_loaded[part], g * 32 + 16 * (b // HALF) + 16)
                        for bk, v in st.drains([], key):
                            pe.wait_ge(drained[bk], v)
                        o = bank[0:k, :].rearrange("p (h q) -> p h q", h=HT)
                        mm(o, kst[part][:, c, b * k:(b + 1) * k], qd[part][:, c, :, b * P:(b + 1) * P], start=True, stop=False)
                        mm(o, pick[part][:], mr[part][:, c * HT:(c + 1) * HT, b % HALF, :], start=False, stop=True)\
                            .then_inc(done, 1)
                    elif work == "pv":
                        b, c = index
                        k = keys[part]
                        last = (part, "pv", (b, NT - 1))
                        sources = [(part, "s2", index)] + ([(part, "v", 0)] if index == (0, 0) else [])
                        for bk, v in st.drains(sources, last if c == 0 else None):
                            pe.wait_ge(drained[bk], v)
                        for j in range(HT):
                            ins = mm(psum[BANK[last]][32 * j:32 * j + VW, c * P:(c + 1) * P], V[part][0:k, b, c * HT + j, :],
                                     probs[0:k, c, j * P:(j + 1) * P], start=True, stop=True)
                        if c == NT - 1:
                            ins.then_inc(filled[BANK[last]], 1)
                    elif work == "oT":
                        transposes(st, key, lambda c: oT[:, c * P:(c + 1) * P], NT, [(part, "pv", (index, NT - 1))])
                    elif work == "nT":
                        transposes(st, key, lambda c: on[:], 1, [(part, "oT", index)])
                    elif work == "wo":
                        for b, v in st.drains([(part, "nT", index)], key):
                            pe.wait_ge(drained[b], v)
                        n = P if part == "A" else UP
                        mm(bank[:, 0:n], onT[:], w["Wo"] if part == "A" else w["wo"], start=True, stop=True).then_inc(done, 1)
                    elif work == "fill" and index[0] == "down":
                        h = DOWN_OF[index[1]]
                        sources = [("M", "fill", ("e1_w2" if h == "e1" else h, k)) for k in range(2)]
                        for b, v in st.drains(sources, key):
                            pe.wait_ge(drained[b], v)
                        for b in range(G):
                            for k in range(2):
                                ins = mm(bank[:, b * UP:(b + 1) * UP], hid[:, HID_AT[h] + k, b * P:(b + 1) * P],
                                         w[f"down{index[1]}"][:, k * UP:(k + 1) * UP], start=k == 0, stop=k == 1)
                        ins.then_inc(done, 1)
                    elif work == "fill" and index[0] in ("e2_l2", "e2_l3", "e3_up"):
                        name, c = index
                        h = {"e2_l2": "e2_l1", "e2_l3": "e2_l2", "e3_up": "e3_down"}[name]
                        chunks = range(1 if name == "e3_up" else 2)
                        for b, v in st.drains([("M", "fill", (h, k)) for k in chunks], key):
                            pe.wait_ge(drained[b], v)
                        for k in chunks:
                            ins = mm(bank[:], w[name][:, k * HID + c * P:k * HID + (c + 1) * P], hid[:, HID_AT[h] + k, :],
                                     start=k == 0, stop=k == chunks[-1])
                        ins.then_inc(done, 1)
                    elif work == "fill":
                        name, c = index
                        for b, v in st.drains([("M", "xfT", 0)], key):
                            pe.wait_ge(drained[b], v)
                        mm(bank[:], w[name][:, c * P:(c + 1) * P], xfT[:], start=True, stop=True).then_inc(done, 1)

            run_steps(pe, step)


def kernel(**inputs):
    import numpy as _np
    import concourse.bacc as _bacc
    from concourse.bass_utils import run_bass_kernel_spmd as _run

    i = {k: _np.asarray(v) for k, v in inputs.items()}
    f = {k.replace("L0_ffn_", ""): v for k, v in i.items() if k.startswith("L0_ffn_")}
    a = {k.replace("L0_xattn_", ""): v for k, v in i.items() if k.startswith("L0_xattn_")}

    def wide(m):
        out = _np.zeros((P, m.shape[1]), m.dtype)
        out[:m.shape[0]] = m
        return out

    def chunks(m):
        return _np.concatenate([m[:P], m[P:]], axis=1)

    parts = {"Wq": a["Wq"], "Wk": wide(a["Wk"]), "Wv": wide(a["Wv"]), "Wo": a["Wo"],
             "wqk": _np.concatenate([f["wq"].T, f["wk"].T], axis=1), "wv": f["wv"].T, "wo": f["wo"].T[:, KEEP:],
             "gate": wide(f["gate_w"]).T, "e0_up": f["e0_up"].T, "e1_w1": f["e1_w1"].T, "e1_w2": f["e1_w2"].T,
             "e2_l1": f["e2_l1"].T, "e2_l2": chunks(f["e2_l2"].T), "e2_l3": chunks(f["e2_l3"].T),
             "e3_down": f["e3_down"].T, "e3_up": f["e3_up"].T,
             "down0": chunks(f["e0_down"].T[:, KEEP:]), "down1": chunks(f["e1_down"].T[:, KEEP:]),
             "down2": chunks(f["e2_l4"].T[:, KEEP:]), "down3": chunks(f["e3_out"].T[:, KEEP:])}
    cols = {"bq": a["bq"], "bk": a["bk"], "n1": f["n1_w"], "n2": f["n2_w"], "qn": _np.tile(f["qn_w"], H),
            "kn": _np.tile(f["kn_w"], H), "gx": _np.repeat(i["g_xattn"], P), "gf": _np.repeat(i["g_ffn"], P)}
    arrays = {
        "x": _np.ascontiguousarray(i["x"]),
        "ctxT": _np.ascontiguousarray(i["ctx_768"].reshape(SEQS * KV, DC).T),
        "weights": _np.ascontiguousarray(_np.concatenate([parts[n] for n, _ in WCOLS], axis=1)),
        "vcols": _np.ascontiguousarray(_np.stack([cols[n] for n in VCOLS], axis=1)),
        "rows": _np.ascontiguousarray(_np.broadcast_to(_np.concatenate([a[n] for n in ROWS]), (P, len(ROWS) * P))),
    }
    nc = _bacc.Bacc("TRN2", target_bir_lowering=False, num_devices=1)
    args = [nc.dram_tensor(f"in_{n}", v.shape, mybir.dt.from_np(v.dtype), kind="ExternalInput").ap() for n, v in arrays.items()]
    o = nc.dram_tensor("out_x", (SEQS, P, P), F32, kind="ExternalOutput").ap()
    build(nc, *args, o)
    r = _run(nc, [{f"in_{n}": v for n, v in arrays.items()}], core_ids=[0])
    return r.results[0]["out_x"]
```

```python
from contextlib import ExitStack

import numpy as np

import concourse.bass as bass
from concourse import mybir

F32 = mybir.dt.float32
BF16 = mybir.dt.bfloat16
F32R = mybir.dt.float32r
ALU = mybir.AluOpType
ACT = mybir.ActivationFunctionType
AX = mybir.AxisListType

P = 128
SEQS = 64
KV = 120
DC = 96
H = 16
HD = 8
E = 4
HID = 256
KEEP = 32
UP = P - KEEP
G = 4
NG = SEQS // G
TOK = G * P
CT = G * KV
HT = 4
NT = H // HT
VW = HD + 1
SPLIT = 3
HIGH_LOW = {"q": (0, 1, 0), "k": (0, 0, 1)}
LN_EPS = 1e-5
RMS_EPS = 1.1920929e-07
SCALE = float(HD) ** -0.5
MASKED = -1e30
F32_MAX = float(np.finfo(np.float32).max)

WCOLS = [("Wq", P), ("Wk", P), ("Wv", P), ("Wo", P), ("wqk", 2 * P), ("wv", P), ("wo", UP), ("gate", P),
         ("e0_up", HID), ("e1_w1", HID), ("e1_w2", HID), ("e2_l1", HID), ("e2_l2", 2 * HID), ("e2_l3", 2 * HID),
         ("e3_down", P), ("e3_up", HID),
         ("down0", 2 * UP), ("down1", 2 * UP), ("down2", 2 * UP), ("down3", 2 * UP)]
VCOLS = ["bq", "bk", "n1", "n2", "qn", "kn", "gx", "gf"]
ROWS = ["bv", "bo"]

M_FILLS = [("e1_w1", 0), ("e1_w2", 0), ("e1_w1", 1), ("e1_w2", 1), ("e2_l1", 0), ("e2_l1", 1), ("e0_up", 0), ("e0_up", 1),
           ("down", 1), ("e2_l2", 0), ("e2_l2", 1), ("down", 0), ("e3_down", 0), ("e2_l3", 0), ("e2_l3", 1),
           ("e3_up", 0), ("e3_up", 1), ("down", 2), ("down", 3)]
HID_AT = {"e1": 0, "e2_l1": 2, "e0_up": 4, "e2_l2": 0, "e3_down": 4, "e2_l3": 2, "e3_up": 0}
DOWN_OF = {0: "e0_up", 1: "e1", 2: "e2_l3", 3: "e3_up"}

RINGS = {"s1": ["s1a", "s1b"], "s2": ["s2a", "s2b"], "x": ["xa", "xb"],
         "pvA": ["pv"], "pvB": ["pv", "s1a"], "tA": ["t"], "tB": ["t", "s1b"]}
BANKS = ["s1a", "s1b", "s2a", "s2b", "xa", "xb", "pv", "t"]
S1B_EARLY = 6


def first_scores():
    a, b = ([(p, "s1", (b, c), "s1") for b in range(G) for c in range(NT)] for p in "AB")
    fills = [("M", "fill", f, "x") for f in M_FILLS]
    between = {
        0: [("M", "squares", 0, None), ("B", "roots", 0, None)],
        1: [("B", "v", 0, "x"), ("M", "norm", 0, None)],
        2: [("B", "scale", 0, None), ("A", "v", 0, "x")],
        3: [("M", "copy", 0, None), ("B", "copy", 0, None), ("B", "qT", 0, "x"), ("B", "kT", 0, "x")],
        4: [("M", "xfT", 0, "x"), ("B", "norm", 0, None)],
        5: [("M", "logits", 0, "x"), fills.pop(0), ("A", "base", 0, None)],
        6: [fills.pop(0)],
        7: [fills.pop(0)],
        8: [fills.pop(0), ("M", "gates", 0, None)],
    }
    for i in range(9, len(a)):
        between[i] = [fills.pop(0)]
    s = []
    for i, tile in enumerate(a):
        s += [tile] + between[i]
    s += [("A", "mT", 0, "x")]
    for i, fill in enumerate(fills):
        s += [fill] + (b[i + S1B_EARLY - len(fills):i + S1B_EARLY - len(fills) + 1] if i >= len(fills) - S1B_EARLY else [])
    return s + [("M", "store", 0, None)]


def second_scores():
    tiles = [(p, b, c) for p in "AB" for b in range(G) for c in range(NT)]
    left = [("B", "s1", (b, c), "s1") for b in range(G) for c in range(NT)][S1B_EARLY:]
    later = {i: [tile] for i, tile in enumerate(left)}
    later[len(left)] = [("B", "mT", 0, "x")]
    later[2].append(("N", "load", 0, None))
    later[3].append(("N", "norm", 0, None))
    later[12] = [("N", "xT", 0, "x")]
    later[14] = [("N", "q", 0, "x")]
    later[16] = [("N", "k", 0, "x")]
    later[17] = [("N", "stacks", 0, None)]
    for i, (p, b, c) in enumerate(tiles):
        later.setdefault(i + 2, []).append((p, "pv", (b, c), "pv" + p if c == NT - 1 else None))
        if c == NT - 1:
            later.setdefault(i + 4, []).append((p, "oT", b, "t" + p))
            later.setdefault(i + 5, []).append((p, "nT", b, "x"))
            later.setdefault(i + 6, []).append((p, "wo", b, "x"))
    n = G * NT + 5
    later[n + 1].append(("A", "stats", 0, None))
    later[n + 4].append(("A", "norm", 0, None))
    later[n + 6].append(("A", "hT", 0, "x"))
    for b in range(G):
        later[n + 7 + b].append(("A", "qk", b, "x"))
    later[n + 10].append(("A", "squares", 0, None))
    s = []
    for i in range(len(tiles) + 6):
        if i < len(tiles):
            p, b, c = tiles[i]
            s.append((p, "s2", (b, c), "s2"))
        s += later.get(i, [])
    return s + [("B", "out", 0, None)]


def schedule_of_a_step():
    return first_scores() + second_scores()


SCHEDULE = schedule_of_a_step()


def bank_of_each_use():
    at, out = dict.fromkeys(RINGS, 0), {}
    for part, work, index, ring in SCHEDULE:
        if ring:
            out[part, work, index] = RINGS[ring][at[ring] % len(RINGS[ring])]
            at[ring] += 1
    return out


BANK = bank_of_each_use()


def uses_before(parts, key=None):
    n = dict.fromkeys(BANKS, 0)
    for part, work, index, ring in SCHEDULE:
        if (part, work, index) == key:
            break
        if ring and part in parts:
            n[BANK[part, work, index]] += 1
    return n


PARTS = "NABM"
RAMP = [(-1, "N"), (0, "NA"), (1, "NAB")]
LOOP = (2, NG - 1)
TAIL = [(NG - 1, "ABM"), (NG, "BM"), (NG + 1, "M")]


class Step:

    def __init__(self, t, parts):
        self.t, self.parts = t, parts
        self.works = [(p, w, i) for p, w, i, _ in SCHEDULE if p in parts]
        self.before = {k: uses_before(parts, k)[BANK[k]] for k in self.works if k in BANK}
        full = uses_before(PARTS)
        self.base = dict.fromkeys(BANKS, 0)
        for t0, p in RAMP + TAIL:
            if parts == PARTS or t0 >= t:
                continue
            for b, n in uses_before(p).items():
                self.base[b] += n
        if parts == PARTS:
            ramp = {b: sum(uses_before(p)[b] for _, p in RAMP) for b in BANKS}
            self.base = {b: t * full[b] + (ramp[b] - LOOP[0] * full[b]) for b in BANKS}
        elif t >= LOOP[1]:
            for b in BANKS:
                self.base[b] += (LOOP[1] - LOOP[0]) * full[b]

    def group(self, part):
        return self.t + 1 - PARTS.index(part)

    def first(self, part):
        return self.parts != PARTS and self.group(part) == 0

    def fills(self, *key):
        return self.base[BANK[key]] + self.before[key] + 1

    def drains(self, sources, fill=None):
        uses = {}
        for key in sources:
            uses[BANK[key]] = max(uses.get(BANK[key], 0), self.before[key] + 1)
        if fill is not None:
            uses[BANK[fill]] = max(uses.get(BANK[fill], 0), self.before[fill])
        pairs = [(bank, self.base[bank] + n) for bank, n in uses.items()]
        return [(bank, n) for bank, n in pairs if not isinstance(n, int) or n > 0]


def run_steps(engine, step):
    for t, parts in RAMP:
        step(Step(t, parts))
    with engine.Fori(*LOOP) as t:
        step(Step(t, PARTS))
    for t, parts in TAIL:
        step(Step(t, parts))


def build(nc, x, ctxT, weights, vcols, rows, out):
    ctx = ExitStack()
    with ctx:
        def sb(name, shape, dt=F32):
            return ctx.enter_context(nc.sbuf_tensor(name, shape, dt))

        def sem(name):
            return ctx.enter_context(nc.semaphore(name))

        psum = {b: ctx.enter_context(nc.psum_tensor(f"ps_{b}", [P, 512], F32)) for b in BANKS}
        filled = {b: sem(f"filled_{b}") for b in BANKS}
        drained = {b: sem(f"drained_{b}") for b in BANKS}

        W = sb("W", [P, sum(n for _, n in WCOLS)])
        at, w = 0, {}
        for name, n in WCOLS:
            w[name] = W[:, at:at + n]
            at += n
        vc = sb("vc", [P, len(VCOLS)])
        col = {n: vc[:, i:i + 1] for i, n in enumerate(VCOLS)}
        rw = sb("rw", [P, len(ROWS) * P])
        bv, bo = rw[:, 0:P], rw[:, P:2 * P]
        tg = sb("tg", [P, 2])
        gx, gf = tg[:, 0:1], tg[:, 1:2]
        qns = sb("qns", [P, 1])
        bqs = sb("bqs", [P, 1])
        gxbo = sb("gxbo", [P, P])
        identf = sb("identf", [P, P])
        identb = sb("identb", [P, P], BF16)
        neg_half = sb("neg_half", [P, G])
        rms_eps = sb("rms_eps", [P, G])
        one = sb("one", [P, 1])
        lower = sb("lower", [P, E * E])
        above = sb("above", [P, 1, P], BF16)

        xt, xn, x1, xy, x2, ym = (sb(n, [P, G, P]) for n in ("xt", "xn", "x1", "xy", "x2", "ym"))
        hb = sb("hb", [P, G, P])
        ctT = sb("ctT", [DC, CT])
        xnT, xfT = (sb(n, [P, TOK]) for n in ("xnT", "xfT"))
        hT = sb("hT", [P, TOK])
        keys = {"A": KV, "B": P}
        whole = sb("whole", [P, TOK])
        xf = sb("xf", [P, G, P])
        split = {o: sb("split_" + o, [P, 2, TOK], F32R) for o in "qk"}
        scratch = {p + o: nc.dram_tensor(f"scratch_{p}{o}", [P * SPLIT, TOK], F32, kind="Internal").ap() for p in "AB" for o in "qk"}
        qTb = {p: sb("qTb" + p, [P, TOK], BF16) for p in "AB"}
        kTb = {p: sb("kTb" + p, [P, G * keys[p]], BF16) for p in "AB"}
        qd = {p: sb("qd" + p, [P, HT, NT, TOK], F32R) for p in "AB"}
        kst = {p: sb("kst" + p, [P, NT, G * keys[p]], F32R) for p in "AB"}
        kd = {p: sb("kd" + p, [P, H, G * keys[p]], BF16) for p in "AB"}
        V = {p: sb("V" + p, [P, G, H, VW]) for p in "AB"}
        mpad = {p: sb("mpad" + p, [P, P]) for p in "AB"}
        mneg = {p: mpad[p][:, 0:G * H].rearrange("p (j c b) -> p j c b", j=HT, c=NT) for p in "AB"}
        mTr = {p: sb("mT" + p, [G * H, P], F32R) for p in "AB"}
        qk = sb("qk", [P, G, 2 * P])
        rden = sb("rden", [P, H])
        on = sb("on", [P, P])
        onT = sb("onT", [P, P])
        hid = sb("hid", [P, 6, TOK])
        sq = sb("sq", [P, G, 2 * P])
        sqM = hid[:, 2].rearrange("p (b d) -> p b d", b=G)
        probs = hid[:, 0:4]
        th, tu = hid[:, 5], hid[:, 4]
        oT = hid[:, 4]
        stA, stB = sb("stA", [P, G, 6]), sb("stB", [P, G, 6])
        mvA, mvB = sb("mvA", [P, G, 2]), sb("mvB", [P, G, 2])
        veA, veB = sb("veA", [P, G]), sb("veB", [P, G])
        rsA = sb("rsA", [P, G])
        rB = sb("rB", [P, 6, G])
        hs, hr = sb("hs", [P, 2 * H * G]), sb("hr", [P, 2 * H * G])
        ssM, msM, rM = sb("ssM", [P, G]), sb("msM", [P, G]), sb("rM", [P, G])
        lg = sb("lg", [P, 8, G, E])
        sm = sb("sm", [P, 5, G])
        cmp = sb("cmp", [P, 2, G, E, E])
        gates = sb("gates", [P, G, E])

        const_loaded = sem("const_loaded")
        setup_dve, setup_pool, setup_act = sem("setup_dve"), sem("setup_pool"), sem("setup_act")
        setup_pool_chain = sem("setup_pool_chain")
        x_loaded, ctx_loaded, stored = sem("x_loaded"), sem("ctx_loaded"), sem("stored")
        kd_loaded = {p: sem("kd_loaded" + p) for p in "AB"}
        stacks_loaded = {p: sem("stacks_loaded" + p) for p in "AB"}
        m_loaded = {p: sem("m_loaded" + p) for p in "AB"}
        cast_ready = {p: sem("cast_ready" + p) for p in "AB"}
        split_ready = {o: sem("split_ready_" + o) for o in "qk"}
        split_stored = {o: sem("split_stored_" + o) for o in "qk"}
        a_stats, a_rstd, xn_ready, x1_base = (sem(n) for n in ("a_stats", "a_rstd", "xn_ready", "x1_base"))
        x1_copied, b_stats, b_pow, b_rs, hb_ready = (sem(n) for n in ("x1_copied", "b_stats", "b_pow", "b_rs", "hb_ready"))
        x2_ready, sq_ready, hs_ready, root_ready, hr_ready, qk_ready = (sem(n) for n in ("x2_ready", "sq_ready", "hs_ready", "root_ready", "hr_ready", "qk_ready"))
        y_ready = sem("y_ready")
        m_sq, m_ms, m_r, xf_ready, y_copied = (sem(n) for n in ("m_sq", "m_ms", "m_r", "xf_ready", "y_copied"))
        gate_step, gate_exp, silu_tanh = (sem(n) for n in ("gate_step", "gate_exp", "silu_tanh"))
        rden_ready = {p: sem("rden_ready" + p) for p in "AB"}

        GROUP_KD, GROUP_STACKS, GROUP_M, USE_STORED = 16 * H, 16 * 2 * HT, 16 * HT, 16 * SPLIT

        def uses_of_split(st, part):
            g = st.group(part)
            if part == "N":
                return 0 if st.first("N") else 2 * g - 1
            return min(2 * g + 2, 2 * NG - 1) if isinstance(g, int) else 2 * g + 2

        SETUP_DVE, SETUP_POOL, SETUP_ACT = 1, 1, 1
        GATE_STEPS = 16
        block = ctx.enter_context(nc.Block())

        @block.sync
        def _(sp):
            sp.dma_start(W[:], weights).then_inc(const_loaded, 16)
            sp.dma_start(vc[:], vcols).then_inc(const_loaded, 16)
            sp.dma_start(rw[:], rows).then_inc(const_loaded, 16)

            def store_split(st, part, to, o):
                n, g = uses_of_split(st, part), st.group(part)
                if not st.first(part):
                    sp.wait_ge(stacks_loaded[to], g * GROUP_STACKS)
                sp.wait_ge(split_ready[o], n * 2 + 2)
                width = G * keys[to] if o == "k" else TOK
                rows3 = scratch[to + o].rearrange("(p s) t -> p s t", s=SPLIT)
                for s in range(SPLIT):
                    sp.dma_start(rows3[:, s, 0:width], split[o][:, HIGH_LOW[o][s], 0:width].bitcast(F32)).then_inc(split_stored[o], 16)

            def load_stacks(st, part, to):
                n = uses_of_split(st, part)
                sp.wait_ge(split_stored["q"], n * USE_STORED + USE_STORED)
                sp.wait_ge(split_stored["k"], n * USE_STORED + USE_STORED)
                rows = HD * SPLIT
                for j in range(HT):
                    at = slice(32 * j, 32 * j + rows)
                    q, k = (scratch[to + o].rearrange("(c j r) t -> j r c t", j=HT, r=rows)[j] for o in "qk")
                    sp.dma_start(qd[to][at, j, :, :].bitcast(F32), q).then_inc(stacks_loaded[to], 16)
                    sp.dma_start(kst[to][at, :, :].bitcast(F32), k[:, :, 0:G * keys[to]]).then_inc(stacks_loaded[to], 16)

            def load_block_diagonal_keys(st, part, to):
                sp.wait_ge(cast_ready[to], st.group(part) * 2 + 2)
                for h in range(H):
                    r = slice(h * HD, h * HD + HD)
                    sp.dma_start(kd[to][r, h, :], kTb[to][r, :]).then_inc(kd_loaded[to], 16)

            def step(st):
                for part, work, index in st.works:
                    g = st.group(part)
                    if (part, work) == ("N", "load"):
                        if not st.first("N"):
                            sp.wait_ge(xn_ready, g)
                            sp.wait_ge(x1_base, g)
                        sp.dma_start(xt[:], x[bass.ds(g * G, G), :, :].rearrange("b t d -> t b d")).then_inc(x_loaded, 16)
                        sp.dma_start(ctT[:], ctxT[:, bass.ds(g * CT, CT)]).then_inc(ctx_loaded, 16)
                    elif (part, work) == ("N", "k"):
                        load_block_diagonal_keys(st, "N", "A")
                        store_split(st, "N", "A", "q")
                        store_split(st, "N", "A", "k")
                        if st.parts == "N":
                            load_stacks(st, "N", "A")
                    elif (part, work) == ("N", "stacks") and st.parts != "N":
                        sp.wait_ge(filled[BANK["A", "s2", (G - 1, NT - 1)]], st.fills("A", "s2", (G - 1, NT - 1)))
                        load_stacks(st, "N", "A")
                    elif (part, work) == ("B", "kT"):
                        load_block_diagonal_keys(st, "B", "B")
                        store_split(st, "B", "B", "q")
                        store_split(st, "B", "B", "k")
                        load_stacks(st, "B", "B")
                    elif work == "mT":
                        sp.wait_ge(drained[BANK[part, "mT", 0]], st.fills(part, "mT", 0))
                        for j in range(HT):
                            row = 32 * j + HD * SPLIT
                            sp.dma_start(qd[part][row:row + 1, j, :, :].rearrange("p c (b q) -> p (c b) q", b=G).bitcast(F32),
                                         mTr[part][j * NT * G:(j + 1) * NT * G, :].bitcast(F32)).then_inc(m_loaded[part], 16)

            sp.wait_ge(setup_pool, SETUP_POOL)
            sp.wait_ge(setup_dve, SETUP_DVE)
            run_steps(sp, step)

        @block.gpsimd
        def _(pool):
            chain = [0]

            def link(ins):
                chain[0] += 1
                ins.then_inc(setup_pool_chain, 1)
                pool.wait_ge(setup_pool_chain, chain[0])

            link(pool.memset(identf[:], 0.0))
            link(pool.affine_select(out=identf[:], in_=identf[:], compare_op=ALU.not_equal, fill=1.0, base=0,
                                    pattern=[[-1, P]], channel_multiplier=1))
            link(pool.tensor_copy(identb[:], identf[:]))
            link(pool.memset(above[:], 0.0))
            link(pool.affine_select(out=above[:], in_=above[:], compare_op=ALU.is_ge, fill=MASKED, base=0,
                                    pattern=[[0, 1], [-1, P]], channel_multiplier=1))
            link(pool.memset(neg_half[:], -0.5))
            link(pool.memset(rms_eps[:], RMS_EPS))
            link(pool.memset(one[:], 1.0))
            link(pool.memset(lower[:], 0.0))
            for e in range(E):
                if e:
                    link(pool.memset(lower[:, e * E:e * E + e], 1.0))
            pool.wait_ge(setup_act, SETUP_ACT)
            link(pool.tensor_tensor(gxbo[:], bo, gx.to_broadcast([P, P]), ALU.mult))
            pool.memset(V["A"][:, :, :, HD:VW], 1.0)
            link(pool.memset(V["B"][:, :, :, HD:VW], 1.0))
            pool.memset(rB[:], 0.0).then_inc(setup_pool, 1)
            pool.wait_ge(setup_pool, 1)
            ones = one[:].rearrange("p (a b) -> p a b", a=1).to_broadcast([P, G, P])

            def step(st):
                for part, work, index in st.works:
                    g = st.group(part)
                    if (part, work) == ("N", "norm"):
                        pool.wait_ge(a_stats, g * 3 + 3)
                        pool.tensor_tensor(rsA[:], veA[:], neg_half[:], ALU.pow).then_inc(a_rstd, 1)
                    elif (part, work) == ("M", "squares"):
                        pool.wait_ge(y_ready, g + 1)
                        pool.tensor_tensor(sqM, x2[:], x2[:], ALU.mult).then_inc(m_sq, 1)
                    elif (part, work) == ("M", "copy"):
                        if not st.first("M"):
                            pool.wait_ge(stored, g * 16)
                        pool.tensor_tensor(ym[:], xy[:], ones, ALU.mult).then_inc(y_copied, 1)
                    elif (part, work) == ("M", "norm"):
                        pool.wait_ge(m_ms, g * 2 + 2)
                        pool.tensor_tensor(rM[:], msM[:], neg_half[:], ALU.pow).then_inc(m_r, 1)
                    elif (part, work) == ("B", "copy"):
                        pool.wait_ge(b_stats, g * 3 + 3)
                        if not st.first("B"):
                            pool.wait_ge(y_copied, g)
                        pool.tensor_tensor(xy[:], x1[:], ones, ALU.mult).then_inc(x1_copied, 1)
                    elif (part, work) == ("A", "stats"):
                        pool.wait_ge(b_stats, g * 3 + 3)
                        pool.tensor_tensor(rB[:, 0], veB[:], neg_half[:], ALU.pow).then_inc(b_pow, 1)
                        pool.wait_ge(b_pow, g * 5 + 1)
                        pool.tensor_tensor(rB[:, 1], rB[:, 0], rB[:, 0], ALU.mult).then_inc(b_pow, 1)
                        pool.wait_ge(b_pow, g * 5 + 2)
                        pool.tensor_tensor(rB[:, 2], rB[:, 1], mvB[:, :, 1], ALU.mult).then_inc(b_pow, 1)
                        pool.wait_ge(b_pow, g * 5 + 3)
                        pool.tensor_tensor(rB[:, 3], rB[:, 2], rms_eps[:], ALU.add).then_inc(b_pow, 1)
                        pool.wait_ge(b_pow, g * 5 + 4)
                        pool.tensor_tensor(rB[:, 4], rB[:, 3], neg_half[:], ALU.pow).then_inc(b_pow, 1)
                        pool.wait_ge(b_pow, g * 5 + 5)
                        pool.tensor_tensor(rB[:, 5], rB[:, 4], rB[:, 0], ALU.mult).then_inc(b_rs, 1)
                    elif (part, work) == ("A", "base"):
                        if not st.first("A"):
                            pool.wait_ge(x2_ready, g)
                            pool.wait_ge(x1_copied, g)
                        pool.wait_ge(x_loaded, g * 16 + 16)
                        pool.tensor_tensor(x1[:], xt[:], gxbo[:].rearrange("p (a d) -> p a d", a=1).to_broadcast([P, G, P]),
                                           ALU.add).then_inc(x1_base, 1)
                    elif (part, work) == ("A", "squares"):
                        for bank, n in st.drains([("A", "qk", b) for b in range(G)]):
                            pool.wait_ge(drained[bank], n)
                        pool.tensor_tensor(sq[:], qk[:], qk[:], ALU.mult).then_inc(sq_ready, 1)
                    elif (part, work) == ("M", "store"):
                        for bank, n in st.drains([("M", "fill", ("down", e)) for e in range(E)]):
                            pool.wait_ge(drained[bank], n)
                        pool.dma_start(out[bass.ds(g * G, G), :, :].rearrange("b t d -> t b d"), ym[:]).then_inc(stored, 16)

            run_steps(pool, step)
            pool.wait_ge(stored, NG * 16)

        @block.scalar
        def _(act):
            act.wait_ge(const_loaded, 48)
            nc.scalar.activation(tg[:], vc[:, len(VCOLS) - 2:len(VCOLS)], ACT.Tanh).then_inc(setup_act, 1)
            act.wait_ge(setup_dve, SETUP_DVE)

            def queries_or_keys(st, part, to, o, **affine):
                key = (part, {"N": o, "B": o + "T"}[part], 0)
                width = G * keys[to] if o == "k" else TOK
                bank = psum[BANK[key]][:, 0:width]
                act.wait_ge(filled[BANK[key]], st.fills(*key))
                nc.scalar.activation((qTb if o == "q" else kTb)[to][:], bank, ACT.Identity, **affine).then_inc(cast_ready[to], 1)
                n = uses_of_split(st, part)
                if o == "k":
                    act.wait_ge(split_ready["q"], n * 2 + 2)
                elif not isinstance(n, int) or n > 0:
                    act.wait_ge(split_ready["k"], n * 2)
                nc.scalar.activation(whole[:, 0:width], bank, ACT.Identity, **affine).then_inc(drained[BANK[key]], 1)

            def step(st):
                for part, work, index in st.works:
                    key, g = (part, work, index), st.group(part)
                    if key in BANK:
                        bank, full, done = psum[BANK[key]], filled[BANK[key]], drained[BANK[key]]
                    if (part, work) == ("N", "xT"):
                        act.wait_ge(full, st.fills(*key))
                        nc.scalar.activation(xnT[:], bank[:], ACT.Copy).then_inc(done, 1)
                    elif (part, work) == ("N", "q"):
                        queries_or_keys(st, "N", "A", "q", bias=bqs[:], scale=SCALE)
                    elif (part, work) == ("N", "k"):
                        queries_or_keys(st, "N", "A", "k", bias=col["bk"])
                    elif (part, work) == ("M", "xfT"):
                        act.wait_ge(full, st.fills(*key))
                        nc.scalar.activation(xfT[:], bank[:], ACT.Identity, scale=col["n2"]).then_inc(done, 1)
                    elif (part, work) == ("A", "hT"):
                        act.wait_ge(full, st.fills(*key))
                        nc.scalar.activation(hT[:], bank[:], ACT.Identity, scale=col["n1"]).then_inc(done, 1)
                    elif (part, work) == ("A", "qk"):
                        act.wait_ge(full, st.fills(*key))
                        nc.scalar.activation(qk[:, index, :], bank[:, 0:2 * P], ACT.Copy).then_inc(done, 1)
                    elif (part, work) == ("B", "v"):
                        act.wait_ge(full, st.fills(*key))
                        nc.scalar.activation(V["B"][:, :, :, 0:HD].rearrange("p b h d -> p (b h) d"),
                                             bank[:].rearrange("p (n d) -> p n d", d=HD), ACT.Copy).then_inc(done, 1)
                    elif (part, work) == ("B", "roots"):
                        act.wait_ge(hs_ready, g * 2 + 2)
                        nc.scalar.activation(hr[:], hs[:], ACT.Sqrt).then_inc(root_ready, 1)
                    elif (part, work) == ("B", "qT"):
                        queries_or_keys(st, "B", "B", "q", scale=qns[:])
                    elif (part, work) == ("B", "kT"):
                        queries_or_keys(st, "B", "B", "k", scale=col["kn"])
                    elif (part, work) == ("M", "gates"):
                        act.wait_ge(gate_step, g * GATE_STEPS + 3)
                        nc.scalar.activation(lg[:, 3], lg[:, 2], ACT.Exp).then_inc(gate_exp, 1)
                    elif work == "mT":
                        act.wait_ge(full, st.fills(*key))
                        nc.scalar.activation(mTr[part][:], bank[0:G * H, 0:P], ACT.Copy).then_inc(done, 1)
                    elif work == "fill" and index[0] == "e1_w1":
                        if index[1]:
                            for b, n in st.drains([("M", "fill", ("e1_w1", index[1] - 1))]):
                                act.wait_ge(drained[b], n)
                        act.wait_ge(full, st.fills(*key))
                        nc.scalar.activation(th, bank[:], ACT.Tanh, scale=0.5).then_inc(silu_tanh, 1)
                    elif work == "fill" and index[0] in HID_AT:
                        if index == ("e0_up", 0):
                            for b, n in st.drains([("M", "fill", ("e1_w1", 1)), ("M", "fill", ("e1_w2", 1))]):
                                act.wait_ge(drained[b], n)
                        act.wait_ge(full, st.fills(*key))
                        nc.scalar.activation(hid[:, HID_AT[index[0]] + index[1], :], bank[:], ACT.Gelu).then_inc(done, 1)
                    elif work == "s2":
                        k = keys[part]
                        act.wait_ge(full, st.fills(*key))
                        nc.scalar.activation(probs[0:k, index[1], :], bank[0:k, :], ACT.Exp).then_inc(done, 1)
                    elif work == "pv" and index[1] == NT - 1:
                        act.wait_ge(full, st.fills(*key))
                        nc.scalar.activation(oT, bank[:], ACT.Copy).then_inc(done, 1)
                    elif work == "nT":
                        act.wait_ge(full, st.fills(*key))
                        nc.scalar.activation(onT[:], bank[:, 0:P], ACT.Copy).then_inc(done, 1)

            run_steps(act, step)

        @block.vector
        def _(dve):
            def statistics(src, stats_of, mv, ve, stats, g):
                for b in range(G):
                    ins = nc.vector.bn_stats(stats_of[:, b, :], src[:, b, :])
                ins.then_inc(stats, 1)
                dve.wait_ge(stats, g * 3 + 1)
                nc.vector.memset(sm[:, 4, 3:4], 0.0)
                for b in range(G):
                    ins = nc.vector.bn_aggr(mv[:, b, :], stats_of[:, b, :])
                ins.then_inc(stats, 1)
                dve.wait_ge(stats, g * 3 + 2)
                nc.vector.tensor_scalar(ve[:], mv[:, :, 1], LN_EPS, None, ALU.add).then_inc(stats, 1)

            def split_rows(st, part, to, o):
                key = (part, {"N": o, "B": o + "T"}[part], 0)
                width = G * keys[to] if o == "k" else TOK
                n = uses_of_split(st, part)
                if not isinstance(n, int) or n > 0:
                    dve.wait_ge(split_stored[o], n * USE_STORED)
                dve.wait_ge(drained[BANK[key]], st.fills(*key))
                nc.vector.tensor_copy(split[o][:, 0, 0:width], whole[:, 0:width]).then_inc(split_ready[o], 1)
                dve.wait_ge(split_ready[o], n * 2 + 1)
                nc.vector.tensor_tensor(split[o][:, 1, 0:width], whole[:, 0:width], split[o][:, 0, 0:width].bitcast(F32),
                                        ALU.subtract).then_inc(split_ready[o], 1)

            def step(st):
                for part, work, index in st.works:
                    key, g = (part, work, index), st.group(part)
                    if key in BANK:
                        bank, full, done = psum[BANK[key]], filled[BANK[key]], drained[BANK[key]]
                    if (part, work) == ("N", "norm"):
                        dve.wait_ge(x_loaded, g * 16 + 16)
                        statistics(xt, stA, mvA, veA, a_stats, g)
                        dve.wait_ge(a_rstd, g + 1)
                        for b in range(G):
                            ins = nc.vector.tensor_scalar(xn[:, b, :], xt[:, b, :], mvA[:, b, 0:1], rsA[:, b:b + 1],
                                                          ALU.subtract, ALU.mult)
                        ins.then_inc(xn_ready, 1)
                    elif (part, work) == ("A", "stats"):
                        for b, n in st.drains([("A", "wo", b) for b in range(G)]):
                            dve.wait_ge(drained[b], n)
                        statistics(x1, stB, mvB, veB, b_stats, g)
                    elif (part, work) == ("A", "norm"):
                        dve.wait_ge(b_rs, g + 1)
                        for b in range(G):
                            ins = nc.vector.tensor_scalar(hb[:, b, :], x1[:, b, :], mvB[:, b, 0:1], rB[:, 5, b:b + 1],
                                                          ALU.subtract, ALU.mult)
                        ins.then_inc(hb_ready, 1)
                    elif (part, work) == ("B", "norm"):
                        if not st.first("B"):
                            dve.wait_ge(xf_ready, g)
                        for b in range(G):
                            ins = nc.vector.tensor_scalar(x2[:, b, :], x1[:, b, :], mvB[:, b, 0:1], rB[:, 0, b:b + 1],
                                                          ALU.subtract, ALU.mult)
                        ins.then_inc(x2_ready, 1)
                    elif (part, work) == ("M", "squares"):
                        dve.wait_ge(m_sq, g + 1)
                        nc.vector.tensor_reduce(ssM[:], sqM, AX.X, ALU.add).then_inc(m_ms, 1)
                        dve.wait_ge(m_ms, g * 2 + 1)
                        nc.vector.tensor_scalar(msM[:], ssM[:], 1.0 / P, RMS_EPS, ALU.mult, ALU.add).then_inc(m_ms, 1)
                    elif (part, work) == ("M", "norm"):
                        dve.wait_ge(m_r, g + 1)
                        for b in range(G):
                            ins = nc.vector.tensor_scalar(xf[:, b, :], x2[:, b, :], rM[:, b:b + 1], None, ALU.mult)
                        ins.then_inc(xf_ready, 1)
                    elif (part, work) in (("N", "q"), ("N", "k")):
                        split_rows(st, "N", "A", work)
                    elif (part, work) in (("B", "qT"), ("B", "kT")):
                        split_rows(st, "B", "B", work[0])
                    elif (part, work) == ("A", "v"):
                        dve.wait_ge(full, st.fills(*key))
                        for b in range(G):
                            ins = nc.vector.tensor_tensor(
                                V["A"][0:KV, b, :, 0:HD], bank[0:KV, b * P:(b + 1) * P].rearrange("p (h d) -> p h d", h=H),
                                bv[0:KV, :].rearrange("p (h d) -> p h d", h=H), ALU.add)
                        ins.then_inc(done, 1)
                    elif (part, work) == ("A", "squares"):
                        dve.wait_ge(sq_ready, g + 1)
                        nc.vector.tensor_reduce(hs[:], sq[:].rearrange("p b (h d) -> p (b h) d", d=HD), AX.X, ALU.add)\
                            .then_inc(hs_ready, 1)
                        dve.wait_ge(hs_ready, g * 2 + 1)
                        nc.vector.tensor_scalar(hs[:], hs[:], 1.0 / HD, RMS_EPS, ALU.mult, ALU.add).then_inc(hs_ready, 1)
                    elif (part, work) == ("B", "scale"):
                        dve.wait_ge(root_ready, g + 1)
                        nc.vector.reciprocal(hr[:], hr[:]).then_inc(hr_ready, 1)
                        dve.wait_ge(hr_ready, g + 1)
                        nc.vector.tensor_tensor(
                            qk[:].rearrange("p b (h d) -> p (b h) d", d=HD), qk[:].rearrange("p b (h d) -> p (b h) d", d=HD),
                            hr[:].rearrange("p (n a) -> p n a", a=1).to_broadcast([P, 2 * H * G, HD]), ALU.mult)\
                            .then_inc(qk_ready, 1)
                    elif (part, work) == ("M", "logits"):
                        logits = bank[:].rearrange("p (b e) -> p b e", b=G)[:, :, 0:E]
                        dve.wait_ge(full, st.fills(*key))
                        nc.vector.tensor_scalar(lg[:, 0], logits, 0.0, F32_MAX, ALU.max, ALU.min)
                        nc.vector.tensor_scalar(lg[:, 1], logits, 0.0, -F32_MAX, ALU.min, ALU.max).then_inc(done, 1)
                    elif (part, work) == ("M", "gates"):
                        choose_experts(st, g)
                    elif work == "s1":
                        b, c = index
                        k = keys[part]
                        dve.wait_ge(full, st.fills(*key))
                        nc.vector.tensor_reduce(mneg[part][:, :, c, b],
                                                bank[:, 0:HT * k].rearrange("p (h k) -> p h k", h=HT),
                                                AX.X, ALU.max, negate=True).then_inc(done, 1)
                    elif work == "fill" and index[0] == "e1_w2":
                        c = index[1]
                        u = BANK["M", "fill", ("e1_w1", c)]
                        if c:
                            for b, n in st.drains([("M", "fill", ("e1_w2", c - 1))]):
                                dve.wait_ge(drained[b], n)
                        dve.wait_ge(silu_tanh, g * 2 + c + 1)
                        nc.vector.scalar_tensor_tensor(out=tu, in0=th, scalar=1.0, in1=psum[u][:],
                                                       op0=ALU.add, op1=ALU.mult).then_inc(drained[u], 1)
                        dve.wait_ge(drained[u], st.fills("M", "fill", ("e1_w1", c)))
                        dve.wait_ge(full, st.fills(*key))
                        nc.vector.scalar_tensor_tensor(out=hid[:, HID_AT["e1"] + c, :], in0=tu, scalar=0.5, in1=bank[:],
                                                       op0=ALU.mult, op1=ALU.mult).then_inc(done, 1)
                    elif work == "fill" and index[0] == "down":
                        e = index[1]
                        order = [f for f in M_FILLS if f[0] == "down"]
                        n = order.index(index)
                        if n == 0:
                            dve.wait_ge(y_copied, g + 1)
                        else:
                            for b, v in st.drains([("M", "fill", order[n - 1])]):
                                dve.wait_ge(drained[b], v)
                        dve.wait_ge(full, st.fills(*key))
                        for b in range(G):
                            ins = nc.vector.scalar_tensor_tensor(
                                out=ym[:, b, KEEP:P], in0=bank[:, b * UP:(b + 1) * UP], scalar=gates[:, b, e:e + 1],
                                in1=ym[:, b, KEEP:P], op0=ALU.mult, op1=ALU.add)
                        ins.then_inc(done, 1)
                    elif work == "oT":
                        dve.wait_ge(full, st.fills(*key))
                        v = bank[:].rearrange("p (h e) -> p h e", h=H)
                        nc.vector.reciprocal(rden[:].rearrange("p (h a) -> p h a", a=1), v[:, :, HD:VW]).then_inc(rden_ready[part], 1)
                        dve.wait_ge(rden_ready[part], g * G + index + 1)
                        nc.vector.tensor_tensor(on[:].rearrange("p (h d) -> p h d", h=H), v[:, :, 0:HD],
                                                rden[:].rearrange("p (h a) -> p h a", a=1).to_broadcast([P, H, HD]),
                                                ALU.mult).then_inc(done, 1)
                    elif work == "wo" and part == "A":
                        if index == 0:
                            dve.wait_ge(x1_base, g + 1)
                        dve.wait_ge(full, st.fills(*key))
                        nc.vector.scalar_tensor_tensor(out=x1[:, index, :], in0=bank[:, 0:P], scalar=gx, in1=x1[:, index, :],
                                                       op0=ALU.mult, op1=ALU.add).then_inc(done, 1)
                    elif work == "wo":
                        dve.wait_ge(full, st.fills(*key))
                        nc.vector.tensor_tensor(x2[:, index, KEEP:P], bank[:, 0:UP], x2[:, index, KEEP:P],
                                                ALU.add).then_inc(done, 1)
                    elif (part, work) == ("B", "out"):
                        for b, n in st.drains([("B", "wo", b) for b in range(G)]):
                            dve.wait_ge(drained[b], n)
                        dve.wait_ge(x1_copied, g + 1)
                        nc.vector.scalar_tensor_tensor(out=xy[:], in0=x2[:], scalar=gf, in1=xy[:],
                                                       op0=ALU.mult, op1=ALU.add).then_inc(y_ready, 1)

            def choose_experts(st, g):
                spot = BANK["M", "logits", 0]
                n = [0]

                def link(ins):
                    ins.then_inc(gate_step, 1)
                    n[0] += 1
                    dve.wait_ge(gate_step, g * GATE_STEPS + n[0])

                def over_experts(a):
                    return a.rearrange("p (b a) -> p b a", a=1).to_broadcast([P, G, E])

                dve.wait_ge(drained[spot], st.fills("M", "logits", 0))
                link(nc.vector.tensor_tensor(lg[:, 4], lg[:, 0], lg[:, 1], ALU.add))
                link(nc.vector.tensor_reduce(sm[:, 0], lg[:, 4], AX.X, ALU.max, negate=True))
                link(nc.vector.tensor_tensor(lg[:, 2], lg[:, 4], over_experts(sm[:, 0]), ALU.add))
                dve.wait_ge(gate_exp, g + 1)
                link(nc.vector.tensor_reduce(sm[:, 1], lg[:, 3], AX.X, ALU.add))
                link(nc.vector.reciprocal(sm[:, 2], sm[:, 1]))
                link(nc.vector.tensor_tensor(lg[:, 5], lg[:, 3], over_experts(sm[:, 2]), ALU.mult))
                p_j = lg[:, 5].rearrange("p b (a e) -> p b a e", a=1).to_broadcast([P, G, E, E])
                p_e = lg[:, 5].rearrange("p b (e a) -> p b e a", a=1).to_broadcast([P, G, E, E])
                for b in range(G):
                    pj, pe_ = p_j[:, b], p_e[:, b]
                    nc.vector.tensor_tensor(cmp[:, 0, b], pj, pe_, ALU.is_gt)
                    last = nc.vector.tensor_tensor(cmp[:, 1, b], pj, pe_, ALU.is_equal)
                link(last)
                link(nc.vector.tensor_tensor(cmp[:, 1].rearrange("p b e j -> p b (e j)"), cmp[:, 1].rearrange("p b e j -> p b (e j)"),
                                             lower[:].rearrange("p (a n) -> p a n", a=1).to_broadcast([P, G, E * E]), ALU.mult))
                link(nc.vector.tensor_tensor(cmp[:, 0].rearrange("p b e j -> p (b e j)"), cmp[:, 0].rearrange("p b e j -> p (b e j)"),
                                             cmp[:, 1].rearrange("p b e j -> p (b e j)"), ALU.add))
                link(nc.vector.tensor_reduce(lg[:, 6], cmp[:, 0], AX.X, ALU.add))
                link(nc.vector.tensor_scalar(lg[:, 7], lg[:, 6], 1.5, None, ALU.is_lt))
                link(nc.vector.tensor_tensor(lg[:, 6], lg[:, 5], lg[:, 7], ALU.mult))
                link(nc.vector.tensor_reduce(sm[:, 3], lg[:, 6], AX.X, ALU.add))
                link(nc.vector.tensor_scalar(sm[:, 1], sm[:, 3], 1e-8, None, ALU.add))
                link(nc.vector.reciprocal(sm[:, 2], sm[:, 1]))
                link(nc.vector.scalar_tensor_tensor(out=gates[:], in0=lg[:, 6], scalar=gf, in1=over_experts(sm[:, 2]),
                                                    op0=ALU.mult, op1=ALU.mult))
                assert n[0] == GATE_STEPS

            for p in "AB":
                nc.vector.memset(qd[p][:].bitcast(F32), 0.0)
                nc.vector.memset(kst[p][:].bitcast(F32), 1.0)
                nc.vector.memset(kd[p][:], 0.0)
                nc.vector.memset(mpad[p][:], 0.0)
            nc.vector.memset(psum["pv"][:], 0.0)
            dve.wait_ge(const_loaded, 48)
            dve.wait_ge(setup_act, SETUP_ACT)
            dve.wait_ge(setup_pool, SETUP_POOL)
            nc.vector.tensor_scalar(bqs[:], col["bq"], SCALE, None, ALU.mult)
            nc.vector.tensor_scalar(qns[:], col["qn"], SCALE, None, ALU.mult).then_inc(setup_dve, 1)
            dve.wait_ge(setup_dve, 1)
            run_steps(dve, step)

        @block.tensor
        def _(pe):
            pe.wait_ge(setup_dve, SETUP_DVE)
            mm = nc.tensor.matmul

            def transposes(st, key, of, n, sources=()):
                for b, v in st.drains(sources, key):
                    pe.wait_ge(drained[b], v)
                for b in range(n):
                    ins = nc.tensor.transpose(psum[BANK[key]][:, b * P:(b + 1) * P], of(b), identf[:])
                ins.then_inc(filled[BANK[key]], 1)

            def step(st):
                for part, work, index in st.works:
                    key, g = (part, work, index), st.group(part)
                    if key in BANK:
                        bank, done = psum[BANK[key]], filled[BANK[key]]
                    if (part, work) == ("N", "xT"):
                        pe.wait_ge(xn_ready, g + 1)
                        transposes(st, key, lambda b: xn[:, b, :], G)
                    elif (part, work) == ("N", "q"):
                        for b, v in st.drains([("N", "xT", 0)], key):
                            pe.wait_ge(drained[b], v)
                        mm(bank[:], w["Wq"], xnT[:], start=True, stop=True).then_inc(done, 1)
                    elif (part, work) == ("N", "k"):
                        pe.wait_ge(ctx_loaded, g * 16 + 16)
                        for b, v in st.drains([], key):
                            pe.wait_ge(drained[b], v)
                        mm(bank[:, 0:CT], w["Wk"][0:DC, :], ctT[:], start=True, stop=True).then_inc(done, 1)
                    elif (part, work) == ("A", "v"):
                        for b, v in st.drains([], key):
                            pe.wait_ge(drained[b], v)
                        for b in range(G):
                            ins = mm(bank[0:KV, b * P:(b + 1) * P], ctT[:, b * KV:(b + 1) * KV], w["Wv"][0:DC, :],
                                     start=True, stop=True)
                        ins.then_inc(done, 1)
                    elif (part, work) == ("M", "xfT"):
                        pe.wait_ge(xf_ready, g + 1)
                        transposes(st, key, lambda b: xf[:, b, :], G)
                    elif (part, work) == ("M", "logits"):
                        for b, v in st.drains([("M", "xfT", 0)], key):
                            pe.wait_ge(drained[b], v)
                        for b in range(G):
                            ins = mm(bank[:, b * P:(b + 1) * P], xfT[:, b * P:(b + 1) * P], w["gate"], start=True, stop=True)
                        ins.then_inc(done, 1)
                    elif (part, work) == ("A", "hT"):
                        pe.wait_ge(hb_ready, g + 1)
                        transposes(st, key, lambda b: hb[:, b, :], G)
                    elif (part, work) == ("A", "qk"):
                        for b, v in st.drains([("A", "hT", 0)], key):
                            pe.wait_ge(drained[b], v)
                        mm(bank[:, 0:2 * P], hT[:, index * P:(index + 1) * P], w["wqk"], start=True, stop=True).then_inc(done, 1)
                    elif (part, work) == ("B", "v"):
                        for b, v in st.drains([], key):
                            pe.wait_ge(drained[b], v)
                        for b in range(G):
                            ins = mm(bank[:, b * P:(b + 1) * P], hT[:, b * P:(b + 1) * P], w["wv"], start=True, stop=True)
                        ins.then_inc(done, 1)
                    elif (part, work) in (("B", "qT"), ("B", "kT")):
                        pe.wait_ge(qk_ready, g + 1)
                        first = 0 if work == "qT" else P
                        transposes(st, key, lambda b: qk[:, b, first:first + P], G)
                    elif work == "s1":
                        b, c = index
                        k = keys[part]
                        if index == (0, 0):
                            pe.wait_ge(cast_ready[part], g * 2 + 2)
                            pe.wait_ge(kd_loaded[part], g * GROUP_KD + GROUP_KD)
                        for bk, v in st.drains([], key):
                            pe.wait_ge(drained[bk], v)
                        o = bank[:, 0:HT * k].rearrange("p (h k) -> p h k", h=HT)
                        ins = mm(o, qTb[part][:, b * P:(b + 1) * P], kd[part][:, c * HT:(c + 1) * HT, b * k:(b + 1) * k],
                                 start=True, stop=part == "A")
                        if part == "B":
                            ins = mm(o, identb[:], above[:].to_broadcast([P, HT, P]), start=False, stop=True)
                        ins.then_inc(done, 1)
                    elif work == "mT":
                        for b, v in st.drains([(part, "s1", (G - 1, NT - 1)), (part, "s1", (G - 1, NT - 2))], key):
                            pe.wait_ge(drained[b], v)
                        nc.tensor.transpose(bank[:, 0:P], mpad[part][:], identf[:]).then_inc(done, 1)
                    elif work == "s2":
                        b, c = index
                        k = keys[part]
                        if index == (0, 0):
                            pe.wait_ge(stacks_loaded[part], g * GROUP_STACKS + GROUP_STACKS)
                            pe.wait_ge(m_loaded[part], g * GROUP_M + GROUP_M)
                        for bk, v in st.drains([], key):
                            pe.wait_ge(drained[bk], v)
                        o = bank[0:k, :].rearrange("p (h q) -> p h q", h=HT)
                        ins = mm(o, kst[part][:, c, b * k:(b + 1) * k], qd[part][:, :, c, b * P:(b + 1) * P],
                                 start=True, stop=part == "A")
                        if part == "B":
                            ins = mm(o, above[:, 0, :], identb[:].rearrange("p (a q) -> p a q", a=1).to_broadcast([P, HT, P]),
                                     start=False, stop=True)
                        ins.then_inc(done, 1)
                    elif work == "pv":
                        b, c = index
                        k = keys[part]
                        last = (part, "pv", (b, NT - 1))
                        sources = [(part, "s2", index)] + ([(part, "v", 0)] if index == (0, 0) else [])
                        for bk, v in st.drains(sources, last if c == 0 else None):
                            pe.wait_ge(drained[bk], v)
                        for j in range(HT):
                            ins = mm(psum[BANK[last]][32 * j:32 * j + VW, c * P:(c + 1) * P], V[part][0:k, b, c * HT + j, :],
                                     probs[0:k, c, j * P:(j + 1) * P], start=True, stop=True)
                        if c == NT - 1:
                            ins.then_inc(filled[BANK[last]], 1)
                    elif work == "oT":
                        transposes(st, key, lambda c: oT[:, c * P:(c + 1) * P], NT, [(part, "pv", (index, NT - 1))])
                    elif work == "nT":
                        transposes(st, key, lambda c: on[:], 1, [(part, "oT", index)])
                    elif work == "wo":
                        for b, v in st.drains([(part, "nT", index)], key):
                            pe.wait_ge(drained[b], v)
                        n = P if part == "A" else UP
                        mm(bank[:, 0:n], onT[:], w["Wo"] if part == "A" else w["wo"], start=True, stop=True).then_inc(done, 1)
                    elif work == "fill" and index[0] == "down":
                        h = DOWN_OF[index[1]]
                        sources = [("M", "fill", ("e1_w2" if h == "e1" else h, k)) for k in range(2)]
                        for b, v in st.drains(sources, key):
                            pe.wait_ge(drained[b], v)
                        for b in range(G):
                            for k in range(2):
                                ins = mm(bank[:, b * UP:(b + 1) * UP], hid[:, HID_AT[h] + k, b * P:(b + 1) * P],
                                         w[f"down{index[1]}"][:, k * UP:(k + 1) * UP], start=k == 0, stop=k == 1)
                        ins.then_inc(done, 1)
                    elif work == "fill" and index[0] in ("e2_l2", "e2_l3", "e3_up"):
                        name, c = index
                        h = {"e2_l2": "e2_l1", "e2_l3": "e2_l2", "e3_up": "e3_down"}[name]
                        chunks = range(1 if name == "e3_up" else 2)
                        for b, v in st.drains([("M", "fill", (h, k)) for k in chunks], key):
                            pe.wait_ge(drained[b], v)
                        for k in chunks:
                            ins = mm(bank[:], w[name][:, k * HID + c * P:k * HID + (c + 1) * P], hid[:, HID_AT[h] + k, :],
                                     start=k == 0, stop=k == chunks[-1])
                        ins.then_inc(done, 1)
                    elif work == "fill":
                        name, c = index
                        for b, v in st.drains([("M", "xfT", 0)], key):
                            pe.wait_ge(drained[b], v)
                        mm(bank[:], w[name][:, c * P:(c + 1) * P], xfT[:], start=True, stop=True).then_inc(done, 1)

            run_steps(pe, step)


def kernel(**inputs):
    import numpy as _np
    import concourse.bacc as _bacc
    from concourse.bass_utils import run_bass_kernel_spmd as _run

    i = {k: _np.asarray(v) for k, v in inputs.items()}
    f = {k.replace("L0_ffn_", ""): v for k, v in i.items() if k.startswith("L0_ffn_")}
    a = {k.replace("L0_xattn_", ""): v for k, v in i.items() if k.startswith("L0_xattn_")}

    def wide(m):
        out = _np.zeros((P, m.shape[1]), m.dtype)
        out[:m.shape[0]] = m
        return out

    def chunks(m):
        return _np.concatenate([m[:P], m[P:]], axis=1)

    parts = {"Wq": a["Wq"], "Wk": wide(a["Wk"]), "Wv": wide(a["Wv"]), "Wo": a["Wo"],
             "wqk": _np.concatenate([f["wq"].T, f["wk"].T], axis=1), "wv": f["wv"].T, "wo": f["wo"].T[:, KEEP:],
             "gate": wide(f["gate_w"]).T, "e0_up": f["e0_up"].T, "e1_w1": f["e1_w1"].T, "e1_w2": f["e1_w2"].T,
             "e2_l1": f["e2_l1"].T, "e2_l2": chunks(f["e2_l2"].T), "e2_l3": chunks(f["e2_l3"].T),
             "e3_down": f["e3_down"].T, "e3_up": f["e3_up"].T,
             "down0": chunks(f["e0_down"].T[:, KEEP:]), "down1": chunks(f["e1_down"].T[:, KEEP:]),
             "down2": chunks(f["e2_l4"].T[:, KEEP:]), "down3": chunks(f["e3_out"].T[:, KEEP:])}
    cols = {"bq": a["bq"], "bk": a["bk"], "n1": f["n1_w"], "n2": f["n2_w"], "qn": _np.tile(f["qn_w"], H),
            "kn": _np.tile(f["kn_w"], H), "gx": _np.repeat(i["g_xattn"], P), "gf": _np.repeat(i["g_ffn"], P)}
    arrays = {
        "x": _np.ascontiguousarray(i["x"]),
        "ctxT": _np.ascontiguousarray(i["ctx_768"].reshape(SEQS * KV, DC).T),
        "weights": _np.ascontiguousarray(_np.concatenate([parts[n] for n, _ in WCOLS], axis=1)),
        "vcols": _np.ascontiguousarray(_np.stack([cols[n] for n in VCOLS], axis=1)),
        "rows": _np.ascontiguousarray(_np.broadcast_to(_np.concatenate([a[n] for n in ROWS]), (P, len(ROWS) * P))),
    }
    nc = _bacc.Bacc("TRN2", target_bir_lowering=False, num_devices=1)
    args = [nc.dram_tensor(f"in_{n}", v.shape, mybir.dt.from_np(v.dtype), kind="ExternalInput").ap() for n, v in arrays.items()]
    o = nc.dram_tensor("out_x", (SEQS, P, P), F32, kind="ExternalOutput").ap()
    build(nc, *args, o)
    r = _run(nc, [{f"in_{n}": v for n, v in arrays.items()}], core_ids=[0])
    return r.results[0]["out_x"]
```

```python
from contextlib import ExitStack

import numpy as np

import concourse.bass as bass
from concourse import mybir

F32 = mybir.dt.float32
BF16 = mybir.dt.bfloat16
F32R = mybir.dt.float32r
ALU = mybir.AluOpType
ACT = mybir.ActivationFunctionType
AX = mybir.AxisListType

P = 128
SEQS = 64
KV = 120
DC = 96
H = 16
HD = 8
E = 4
HID = 256
KEEP = 32
UP = P - KEEP
G = 4
NG = SEQS // G
TOK = G * P
CT = G * KV
HT = 4
NT = H // HT
VW = HD + 1
SPLIT = 3
HIGH_LOW = {"q": (0, 1, 0), "k": (0, 0, 1)}
LN_EPS = 1e-5
RMS_EPS = 1.1920929e-07
SCALE = float(HD) ** -0.5
MASKED = -1e30
F32_MAX = float(np.finfo(np.float32).max)

WCOLS = [("Wq", P), ("Wk", P), ("Wv", P), ("Wo", P), ("wqk", 2 * P), ("wv", P), ("wo", UP), ("gate", P),
         ("e0_up", HID), ("e1_w1", HID), ("e1_w2", HID), ("e2_l1", HID), ("e2_l2", 2 * HID), ("e2_l3", 2 * HID),
         ("e3_down", P), ("e3_up", HID),
         ("down0", 2 * UP), ("down1", 2 * UP), ("down2", 2 * UP), ("down3", 2 * UP)]
VCOLS = ["bv", "bq", "bk", "n1", "n2", "qn", "kn", "gx", "gf"]
ROWS = ["bo"]

M_FILLS = [("e1_w1", 0), ("e1_w2", 0), ("e1_w1", 1), ("e1_w2", 1), ("e2_l1", 0), ("e2_l1", 1), ("e0_up", 0), ("e0_up", 1),
           ("e2_l2", 0), ("e2_l2", 1), ("e3_down", 0), ("down", 1), ("e2_l3", 0), ("e2_l3", 1), ("down", 0),
           ("e3_up", 0), ("e3_up", 1)]
LATE_FILLS = [("down", 2), ("down", 3)]
HID_AT = {"e1": 0, "e2_l1": 2, "e0_up": 4, "e2_l2": 8, "e3_down": 2, "e2_l3": 6, "e3_up": 8}
DOWN_OF = {0: "e0_up", 1: "e1", 2: "e2_l3", 3: "e3_up"}

RINGS = {"s1": ["s1a", "s1b"], "s2": ["s2a", "s2b"], "x": ["xa", "xb"],
         "x4": ["xa", "xb", "t", "pv"],
         "pvA": ["pv"], "n": ["s1b", "s1a"], "pvB": ["s1a", "pv"], "tA": ["t"], "tB": ["t", "s1b"]}
BANKS = ["s1a", "s1b", "s2a", "s2b", "xa", "xb", "pv", "t"]
S1B_EARLY = 5


def first_scores():
    a, b = ([(p, "s1", (b, c), "s1") for b in range(G) for c in range(NT)] for p in "AB")
    fills = [("M", "fill", f, "x4") for f in M_FILLS]
    between = {
        0: [("M", "squares", 0, None), ("L", "fill", LATE_FILLS[0], "x4")],
        1: [("B", "v", 0, "x4"), ("B", "qT", 0, "x4")],
        2: [("B", "kT", 0, "x4"), ("M", "norm", 0, None), ("L", "fill", LATE_FILLS[1], "x4")],
        3: [("M", "xfT", 0, "x4")],
        4: [("B", "norm", 0, None), ("M", "logits", 0, "x4"), fills.pop(0), fills.pop(0)],
        5: [("L", "store", 0, None), fills.pop(0), fills.pop(0), ("M", "gates", 0, None)],
        6: [fills.pop(0)],
        7: [fills.pop(0)],
        8: [("M", "gates", 1, None), fills.pop(0)],
        9: [fills.pop(0)],
        10: [("M", "gates", 2, None), fills.pop(0), ("M", "copy", 0, None), ("B", "copy", 0, None)],
        11: [fills.pop(0)],
        12: [("M", "gates", 3, None), fills.pop(0), ("A", "base", 0, None)],
        13: [("M", "gates", 4, None), fills.pop(0)],
    }
    for i in range(14, len(a)):
        between[i] = [fills.pop(0)]
    s = []
    for i, tile in enumerate(a):
        s += [tile] + between[i]
    s += [("A", "mT", 0, "x4"), ("N", "load", 0, None)]
    left = S1B_EARLY
    for i, fill in enumerate(fills):
        n = left // (len(fills) - i)
        s += [fill] + b[S1B_EARLY - left:S1B_EARLY - left + n]
        left -= n
    return s


def second_scores():
    tiles = [(p, b, c) for p in "AB" for b in range(G) for c in range(NT)]
    left = [("B", "s1", (b, c), "s1") for b in range(G) for c in range(NT)][S1B_EARLY:]
    later = {i: [tile] for i, tile in enumerate(left)}
    later[len(left)] = [("B", "mT", 0, "x")]
    later[4].append(("N", "stats", 0, None))
    later.setdefault(8, []).append(("N", "norm", 0, None))
    later[12] = [("N", "xT", 0, "n")]
    later[14] = [("N", "q", 0, "n")]
    later[16] = [("N", "k", 0, "n")]
    later[17] = [("N", "stacks", 0, None)]
    for i, (p, b, c) in enumerate(tiles):
        later.setdefault(i + 2, []).append((p, "pv", (b, c), "pv" + p if c == NT - 1 else None))
        if c == NT - 1:
            later.setdefault(i + 4, []).append((p, "oT", b, "t" + p))
            late = p == "A" and b < G - 1
            later.setdefault(i + 5 + late, []).append((p, "nT", b, "x"))
            later.setdefault(i + 6 + late, []).append((p, "wo", b, "x"))
    n = G * NT + 5
    later[n + 1].append(("A", "stats", 0, None))
    later[n + 4].append(("A", "norm", 0, None))
    later[n + 6].append(("A", "hT", 0, "x"))
    for b in range(G):
        later[n + 7 + b].append(("A", "qk", b, "x"))
    later[n + 10].append(("A", "squares", 0, None))
    later.setdefault(n + 13, []).append(("N", "v", 0, "x"))
    later.setdefault(n + 15, []).append(("A", "sums", 0, None))
    s = []
    for i in range(len(tiles) + 6):
        if i < len(tiles):
            p, b, c = tiles[i]
            s.append((p, "s2", (b, c), "s2"))
        s += later.get(i, [])
    return s + [("B", "out", 0, None), ("A", "scale", 0, None)]


def schedule_of_a_step():
    return first_scores() + second_scores()


SCHEDULE = schedule_of_a_step()


def bank_of_each_use():
    at, out = dict.fromkeys(RINGS, 0), {}
    for part, work, index, ring in SCHEDULE:
        if ring:
            out[part, work, index] = RINGS[ring][at[ring] % len(RINGS[ring])]
            at[ring] += 1
    return out


BANK = bank_of_each_use()


def uses_before(parts, key=None):
    n = dict.fromkeys(BANKS, 0)
    for part, work, index, ring in SCHEDULE:
        if (part, work, index) == key:
            break
        if ring and part in parts:
            n[BANK[part, work, index]] += 1
    return n


PARTS = "NABML"
RAMP = [(-1, "N"), (0, "NA"), (1, "NAB"), (2, "NABM")]
LOOP = (3, NG - 1)
TAIL = [(NG - 1, "ABML"), (NG, "BML"), (NG + 1, "ML"), (NG + 2, "L")]


class Step:

    def __init__(self, t, parts):
        self.t, self.parts = t, parts
        self.works = [(p, w, i) for p, w, i, _ in SCHEDULE if p in parts]
        self.before = {k: uses_before(parts, k)[BANK[k]] for k in self.works if k in BANK}
        full = uses_before(PARTS)
        self.base = dict.fromkeys(BANKS, 0)
        for t0, p in RAMP + TAIL:
            if parts == PARTS or t0 >= t:
                continue
            for b, n in uses_before(p).items():
                self.base[b] += n
        if parts == PARTS:
            ramp = {b: sum(uses_before(p)[b] for _, p in RAMP) for b in BANKS}
            self.base = {b: t * full[b] + (ramp[b] - LOOP[0] * full[b]) for b in BANKS}
        elif t >= LOOP[1]:
            for b in BANKS:
                self.base[b] += (LOOP[1] - LOOP[0]) * full[b]

    def group(self, part):
        return self.t + 1 - PARTS.index(part)

    def first(self, part):
        return self.parts != PARTS and self.group(part) == 0

    def fills(self, *key):
        return self.base[BANK[key]] + self.before[key] + 1

    def drains(self, sources, fill=None):
        uses = {}
        for key in sources:
            uses[BANK[key]] = max(uses.get(BANK[key], 0), self.before[key] + 1)
        if fill is not None:
            uses[BANK[fill]] = max(uses.get(BANK[fill], 0), self.before[fill])
        pairs = [(bank, self.base[bank] + n) for bank, n in uses.items()]
        return [(bank, n) for bank, n in pairs if not isinstance(n, int) or n > 0]


def run_steps(engine, step):
    for t, parts in RAMP:
        step(Step(t, parts))
    with engine.Fori(*LOOP) as t:
        step(Step(t, PARTS))
    for t, parts in TAIL:
        step(Step(t, parts))


def build(nc, x, ctxT, weights, vcols, rows, out):
    ctx = ExitStack()
    with ctx:
        def sb(name, shape, dt=F32):
            return ctx.enter_context(nc.sbuf_tensor(name, shape, dt))

        def sem(name):
            return ctx.enter_context(nc.semaphore(name))

        psum = {b: ctx.enter_context(nc.psum_tensor(f"ps_{b}", [P, 512], F32)) for b in BANKS}
        filled = {b: sem(f"filled_{b}") for b in BANKS}
        drained = {b: sem(f"drained_{b}") for b in BANKS}

        W = sb("W", [P, sum(n for _, n in WCOLS)])
        at, w = 0, {}
        for name, n in WCOLS:
            w[name] = W[:, at:at + n]
            at += n
        vc = sb("vc", [P, len(VCOLS)])
        col = {n: vc[:, i:i + 1] for i, n in enumerate(VCOLS)}
        rw = sb("rw", [P, len(ROWS) * P])
        bo = rw[:]
        tg = sb("tg", [P, 2])
        gx, gf = tg[:, 0:1], tg[:, 1:2]
        qns = sb("qns", [P, 1])
        gxbo = sb("gxbo", [P, P])
        identf = sb("identf", [P, P])
        identb = sb("identb", [P, P], BF16)
        neg_half = sb("neg_half", [P, G])
        rms_eps = sb("rms_eps", [P, G])
        one = sb("one", [P, 1])
        lower = sb("lower", [P, E * E])
        above = sb("above", [P, 1, P], BF16)

        xt, xn, x1, xy, x2, ym = (sb(n, [P, G, P]) for n in ("xt", "xn", "x1", "xy", "x2", "ym"))
        hb = sb("hb", [P, G, P])
        ctT = sb("ctT", [DC, CT])
        xnT, xfT = (sb(n, [P, TOK]) for n in ("xnT", "xfT"))
        hT = sb("hT", [P, TOK])
        keys = {"A": KV, "B": P}
        xf = sb("xf", [P, G, P])
        split = {o: sb("split_" + o, [P, 2, TOK], F32R) for o in "qk"}
        scratch = {p + o: nc.dram_tensor(f"scratch_{p}{o}", [P * SPLIT, TOK], F32, kind="Internal").ap() for p in "AB" for o in "qk"}
        qTb = {p: sb("qTb" + p, [P, TOK], BF16) for p in "AB"}
        kTb = {p: sb("kTb" + p, [P, G * keys[p]], BF16) for p in "AB"}
        qd = {p: sb("qd" + p, [P, HT, NT, TOK], F32R) for p in "AB"}
        kst = {p: sb("kst" + p, [P, NT, G * keys[p]], F32R) for p in "AB"}
        kd = {p: sb("kd" + p, [P, H, G * keys[p]], BF16) for p in "AB"}
        V = {p: sb("V" + p, [P, G, H, VW]) for p in "AB"}
        mpad = {p: sb("mpad" + p, [P, P]) for p in "AB"}
        mneg = {p: mpad[p][:, 0:G * H].rearrange("p (j c b) -> p j c b", j=HT, c=NT) for p in "AB"}
        mTr = {p: sb("mT" + p, [G * H, P], F32R) for p in "AB"}
        qk = sb("qk", [P, G, 2 * P])
        rden = sb("rden", [P, H])
        on = sb("on", [P, P])
        onT = sb("onT", [P, P])
        hid = sb("hid", [P, 10, TOK])
        sq = sb("sq", [P, G, 2 * P])
        sqM = hid[:, 2].rearrange("p (b d) -> p b d", b=G)
        probs = hid[:, 0:4]
        th, tu = hid[:, 5], hid[:, 4]
        oT = hid[:, 4]
        stA, stB = sb("stA", [P, G, 6]), sb("stB", [P, G, 6])
        mvA, mvB = sb("mvA", [P, G, 2]), sb("mvB", [P, G, 2])
        veA, veB = sb("veA", [P, G]), sb("veB", [P, G])
        rsA = sb("rsA", [P, G])
        rB = sb("rB", [P, 6, G])
        hs, hr = sb("hs", [P, 2 * H * G]), sb("hr", [P, 2 * H * G])
        ssM, msM, rM = sb("ssM", [P, G]), sb("msM", [P, G]), sb("rM", [P, G])
        lg = sb("lg", [P, 8, G, E])
        sm = sb("sm", [P, 5, G])
        cmp = sb("cmp", [P, 2, G, E, E])
        gates = sb("gates", [P, G, E])

        const_loaded = sem("const_loaded")
        a_cleared, b_cleared = sem("a_cleared"), sem("b_cleared")
        setup_pe, bias_ready = sem("setup_pe"), sem("bias_ready")
        setup_dve, setup_pool, setup_act = sem("setup_dve"), sem("setup_pool"), sem("setup_act")
        setup_pool_chain = sem("setup_pool_chain")
        x_loaded, ctx_loaded, stored = sem("x_loaded"), sem("ctx_loaded"), sem("stored")
        kd_loaded = {p: sem("kd_loaded" + p) for p in "AB"}
        stacks_loaded = {p: sem("stacks_loaded" + p) for p in "AB"}
        m_loaded = {p: sem("m_loaded" + p) for p in "AB"}
        cast_ready = {p: sem("cast_ready" + p) for p in "AB"}
        high_ready = {o: sem("high_ready_" + o) for o in "qk"}
        split_stored = {o: sem("split_stored_" + o) for o in "qk"}
        a_stats, a_rstd, xn_ready, x1_base = (sem(n) for n in ("a_stats", "a_rstd", "xn_ready", "x1_base"))
        x1_copied, b_stats, b_pow, b_rs, hb_ready = (sem(n) for n in ("x1_copied", "b_stats", "b_pow", "b_rs", "hb_ready"))
        x2_ready, sq_ready, hs_ready, root_ready, hr_ready, qk_ready = (sem(n) for n in ("x2_ready", "sq_ready", "hs_ready", "root_ready", "hr_ready", "qk_ready"))
        y_ready = sem("y_ready")
        m_sq, m_ms, m_r, xf_ready, y_copied = (sem(n) for n in ("m_sq", "m_ms", "m_r", "xf_ready", "y_copied"))
        gate_step, gate_exp, silu_tanh = (sem(n) for n in ("gate_step", "gate_exp", "silu_tanh"))
        rden_ready = {p: sem("rden_ready" + p) for p in "AB"}

        GROUP_KD, GROUP_STACKS, GROUP_M, USE_STORED = 16 * H, 16 * 2 * HT, 16 * HT, 16 * SPLIT

        def uses_of_split(st, part):
            g = st.group(part)
            if part == "N":
                return 0 if st.first("N") else 2 * g - 1
            return min(2 * g + 2, 2 * NG - 1) if isinstance(g, int) else 2 * g + 2

        SETUP_DVE, SETUP_POOL, SETUP_ACT = 1, 1, 1
        GATE_STEPS = 16
        block = ctx.enter_context(nc.Block())

        @block.sync
        def _(sp):
            sp.dma_start(vc[:], vcols).then_inc(const_loaded, 16)
            sp.dma_start(rw[:], rows).then_inc(const_loaded, 16)
            sp.dma_start(W[:], weights).then_inc(const_loaded, 16)

            def store_split(st, part, to, o):
                key = (part, {"N": o, "B": o + "T"}[part], 0)
                sp.wait_ge(drained[BANK[key]], st.fills(*key))
                width = G * keys[to] if o == "k" else TOK
                rows3 = scratch[to + o].rearrange("(p s) t -> p s t", s=SPLIT)
                for s in range(SPLIT):
                    sp.dma_start(rows3[:, s, 0:width], split[o][:, HIGH_LOW[o][s], 0:width].bitcast(F32)).then_inc(split_stored[o], 16)

            def load_stacks(st, part, to):
                n = uses_of_split(st, part)
                sp.wait_ge(split_stored["q"], n * USE_STORED + USE_STORED)
                sp.wait_ge(split_stored["k"], n * USE_STORED + USE_STORED)
                rows = HD * SPLIT
                for j in range(HT):
                    at = slice(32 * j, 32 * j + rows)
                    q, k = (scratch[to + o].rearrange("(c j r) t -> j r c t", j=HT, r=rows)[j] for o in "qk")
                    sp.dma_start(qd[to][at, j, :, :].bitcast(F32), q).then_inc(stacks_loaded[to], 16)
                    sp.dma_start(kst[to][at, :, :].bitcast(F32), k[:, :, 0:G * keys[to]]).then_inc(stacks_loaded[to], 16)

            def load_block_diagonal_keys(st, part, to):
                sp.wait_ge(cast_ready[to], st.group(part) * 2 + 2)
                for h in range(H):
                    r = slice(h * HD, h * HD + HD)
                    sp.dma_start(kd[to][r, h, :], kTb[to][r, :]).then_inc(kd_loaded[to], 16)

            def step(st):
                for part, work, index in st.works:
                    g = st.group(part)
                    if (part, work) == ("N", "load"):
                        if not st.first("N"):
                            sp.wait_ge(xn_ready, g)
                            sp.wait_ge(x1_base, g)
                        sp.dma_start(xt[:], x[bass.ds(g * G, G), :, :].rearrange("b t d -> t b d")).then_inc(x_loaded, 16)
                        sp.dma_start(ctT[:], ctxT[:, bass.ds(g * CT, CT)]).then_inc(ctx_loaded, 16)
                    elif (part, work) == ("N", "k"):
                        if st.parts == "N":
                            sp.wait_ge(setup_dve, SETUP_DVE)
                        load_block_diagonal_keys(st, "N", "A")
                        store_split(st, "N", "A", "q")
                        store_split(st, "N", "A", "k")
                        if st.parts == "N":
                            sp.wait_ge(a_cleared, 1)
                            load_stacks(st, "N", "A")
                    elif (part, work) == ("N", "stacks") and st.parts != "N":
                        sp.wait_ge(filled[BANK["A", "s2", (G - 1, NT - 1)]], st.fills("A", "s2", (G - 1, NT - 1)))
                        load_stacks(st, "N", "A")
                    elif (part, work) == ("B", "kT"):
                        if st.first("B"):
                            sp.wait_ge(b_cleared, 1)
                        load_block_diagonal_keys(st, "B", "B")
                        store_split(st, "B", "B", "q")
                        store_split(st, "B", "B", "k")
                        load_stacks(st, "B", "B")
                    elif work == "mT":
                        sp.wait_ge(drained[BANK[part, "mT", 0]], st.fills(part, "mT", 0))
                        for j in range(HT):
                            row = 32 * j + HD * SPLIT
                            sp.dma_start(qd[part][row:row + 1, j, :, :].rearrange("p c (b q) -> p (c b) q", b=G).bitcast(F32),
                                         mTr[part][j * NT * G:(j + 1) * NT * G, :].bitcast(F32)).then_inc(m_loaded[part], 16)

            run_steps(sp, step)

        @block.gpsimd
        def _(pool):
            chain = [0]

            def link(ins):
                chain[0] += 1
                ins.then_inc(setup_pool_chain, 1)
                pool.wait_ge(setup_pool_chain, chain[0])

            link(pool.memset(identf[:], 0.0))
            link(pool.affine_select(out=identf[:], in_=identf[:], compare_op=ALU.not_equal, fill=1.0, base=0,
                                    pattern=[[-1, P]], channel_multiplier=1))
            link(pool.tensor_copy(identb[:], identf[:]))
            link(pool.memset(above[:], 0.0))
            link(pool.affine_select(out=above[:], in_=above[:], compare_op=ALU.is_ge, fill=MASKED, base=0,
                                    pattern=[[0, 1], [-1, P]], channel_multiplier=1))
            link(pool.memset(neg_half[:], -0.5))
            link(pool.memset(rms_eps[:], RMS_EPS))
            link(pool.memset(one[:], 1.0))
            link(pool.memset(lower[:], 0.0))
            for e in range(E):
                if e:
                    link(pool.memset(lower[:, e * E:e * E + e], 1.0))
            pool.wait_ge(setup_act, SETUP_ACT)
            pool.memset(V["A"][:, :, :, HD:VW], 1.0)
            link(pool.memset(V["B"][:, :, :, HD:VW], 1.0))
            pool.memset(rB[:], 0.0).then_inc(setup_pool, 1)
            pool.wait_ge(setup_pool, 1)
            pool.wait_ge(bias_ready, 2)
            ones = one[:].rearrange("p (a b) -> p a b", a=1).to_broadcast([P, G, P])

            def step(st):
                for part, work, index in st.works:
                    g = st.group(part)
                    if (part, work) == ("N", "norm"):
                        pool.wait_ge(a_stats, g * 3 + 3)
                        pool.tensor_tensor(rsA[:], veA[:], neg_half[:], ALU.pow).then_inc(a_rstd, 1)
                        if st.parts == "N":
                            pool.memset(kd["B"][:], 0.0)
                            pool.memset(qd["B"][:].bitcast(F32), 0.0)
                            pool.memset(kst["B"][:].bitcast(F32), 1.0).then_inc(b_cleared, 1)
                    elif (part, work) == ("M", "squares"):
                        pool.wait_ge(y_ready, g + 1)
                        pool.tensor_tensor(sqM, x2[:], x2[:], ALU.mult).then_inc(m_sq, 1)
                    elif (part, work) == ("M", "copy"):
                        if not st.first("M"):
                            pool.wait_ge(stored, g * 16)
                        pool.tensor_tensor(ym[:], xy[:], ones, ALU.mult).then_inc(y_copied, 1)
                    elif (part, work) == ("M", "norm"):
                        pool.wait_ge(m_ms, g * 2 + 2)
                        pool.tensor_tensor(rM[:], msM[:], neg_half[:], ALU.pow).then_inc(m_r, 1)
                    elif (part, work) == ("B", "copy"):
                        pool.wait_ge(b_stats, g * 3 + 3)
                        if not st.first("B"):
                            pool.wait_ge(y_copied, g)
                        pool.tensor_tensor(xy[:], x1[:], ones, ALU.mult).then_inc(x1_copied, 1)
                    elif (part, work) == ("A", "stats"):
                        pool.wait_ge(b_stats, g * 3 + 3)
                        pool.tensor_tensor(rB[:, 0], veB[:], neg_half[:], ALU.pow).then_inc(b_pow, 1)
                        pool.wait_ge(b_pow, g * 5 + 1)
                        pool.tensor_tensor(rB[:, 1], rB[:, 0], rB[:, 0], ALU.mult).then_inc(b_pow, 1)
                        pool.wait_ge(b_pow, g * 5 + 2)
                        pool.tensor_tensor(rB[:, 2], rB[:, 1], mvB[:, :, 1], ALU.mult).then_inc(b_pow, 1)
                        pool.wait_ge(b_pow, g * 5 + 3)
                        pool.tensor_tensor(rB[:, 3], rB[:, 2], rms_eps[:], ALU.add).then_inc(b_pow, 1)
                        pool.wait_ge(b_pow, g * 5 + 4)
                        pool.tensor_tensor(rB[:, 4], rB[:, 3], neg_half[:], ALU.pow).then_inc(b_pow, 1)
                        pool.wait_ge(b_pow, g * 5 + 5)
                        pool.tensor_tensor(rB[:, 5], rB[:, 4], rB[:, 0], ALU.mult).then_inc(b_rs, 1)
                    elif (part, work) == ("A", "base"):
                        if not st.first("A"):
                            pool.wait_ge(x2_ready, g)
                            pool.wait_ge(x1_copied, g)
                        pool.wait_ge(x_loaded, g * 16 + 16)
                        pool.tensor_tensor(x1[:], xt[:], gxbo[:].rearrange("p (a d) -> p a d", a=1).to_broadcast([P, G, P]),
                                           ALU.add).then_inc(x1_base, 1)
                    elif (part, work) == ("A", "squares"):
                        for bank, n in st.drains([("A", "qk", b) for b in range(G)]):
                            pool.wait_ge(drained[bank], n)
                        pool.tensor_tensor(sq[:], qk[:], qk[:], ALU.mult).then_inc(sq_ready, 1)
            run_steps(pool, step)

        @block.scalar
        def _(act):
            act.wait_ge(const_loaded, 48)
            nc.scalar.activation(tg[:], vc[:, len(VCOLS) - 2:len(VCOLS)], ACT.Tanh).then_inc(setup_act, 1)
            act.wait_ge(setup_dve, SETUP_DVE)

            def queries_or_keys(st, part, to, o, **affine):
                key = (part, {"N": o, "B": o + "T"}[part], 0)
                width = G * keys[to] if o == "k" else TOK
                bank = psum[BANK[key]][:, 0:width]
                act.wait_ge(filled[BANK[key]], st.fills(*key))
                nc.scalar.activation((qTb if o == "q" else kTb)[to][:], bank, ACT.Identity, **affine).then_inc(cast_ready[to], 1)
                n = uses_of_split(st, part)
                if not isinstance(n, int) or n > 0:
                    act.wait_ge(split_stored[o], n * USE_STORED)
                nc.scalar.activation(split[o][:, 0, 0:width], bank, ACT.Identity, **affine).then_inc(high_ready[o], 1)

            def step(st):
                for part, work, index in st.works:
                    key, g = (part, work, index), st.group(part)
                    if key in BANK:
                        bank, full, done = psum[BANK[key]], filled[BANK[key]], drained[BANK[key]]
                    if (part, work) == ("N", "xT"):
                        act.wait_ge(full, st.fills(*key))
                        nc.scalar.activation(xnT[:], bank[:], ACT.Copy).then_inc(done, 1)
                    elif (part, work) == ("N", "q"):
                        queries_or_keys(st, "N", "A", "q", bias=col["bq"])
                    elif (part, work) == ("N", "k"):
                        queries_or_keys(st, "N", "A", "k", bias=col["bk"])
                    elif (part, work) == ("L", "store"):
                        act.wait_ge(drained[BANK["L", "fill", LATE_FILLS[1]]], st.fills("L", "fill", LATE_FILLS[1]))
                        act.dma_start(out[bass.ds(g * G, G), :, :].rearrange("b t d -> t b d"), ym[:]).then_inc(stored, 16)
                    elif (part, work) == ("M", "norm"):
                        act.wait_ge(m_r, g + 1)
                        for b in range(G):
                            ins = nc.scalar.activation(xf[:, b, :], x2[:, b, :], ACT.Copy, scale=rM[:, b:b + 1])
                        ins.then_inc(xf_ready, 1)
                    elif (part, work) == ("M", "xfT"):
                        act.wait_ge(full, st.fills(*key))
                        nc.scalar.activation(xfT[:], bank[:], ACT.Identity, scale=col["n2"]).then_inc(done, 1)
                    elif (part, work) == ("N", "v"):
                        act.wait_ge(full, st.fills(*key))
                        nc.scalar.activation(V["A"][0:KV, :, :, 0:HD].rearrange("p b h d -> p (b h) d"),
                                             bank[0:KV, :].rearrange("p (n d) -> p n d", d=HD), ACT.Copy).then_inc(done, 1)
                    elif (part, work) == ("A", "hT"):
                        act.wait_ge(full, st.fills(*key))
                        nc.scalar.activation(hT[:], bank[:], ACT.Identity, scale=col["n1"]).then_inc(done, 1)
                    elif (part, work) == ("A", "qk"):
                        act.wait_ge(full, st.fills(*key))
                        nc.scalar.activation(qk[:, index, :], bank[:, 0:2 * P], ACT.Copy).then_inc(done, 1)
                    elif (part, work) == ("B", "v"):
                        act.wait_ge(full, st.fills(*key))
                        nc.scalar.activation(V["B"][:, :, :, 0:HD].rearrange("p b h d -> p (b h) d"),
                                             bank[:].rearrange("p (n d) -> p n d", d=HD), ACT.Copy).then_inc(done, 1)
                    elif (part, work) == ("A", "sums"):
                        act.wait_ge(hs_ready, g * 2 + 2)
                        nc.scalar.activation(hr[:], hs[:], ACT.Sqrt).then_inc(root_ready, 1)
                    elif (part, work) == ("B", "qT"):
                        queries_or_keys(st, "B", "B", "q", scale=qns[:])
                    elif (part, work) == ("B", "kT"):
                        queries_or_keys(st, "B", "B", "k", scale=col["kn"])
                    elif (part, work, index) == ("M", "gates", 0):
                        act.wait_ge(gate_step, g * GATE_STEPS + 3)
                        nc.scalar.activation(lg[:, 3], lg[:, 2], ACT.Exp).then_inc(gate_exp, 1)
                    elif work == "mT":
                        act.wait_ge(full, st.fills(*key))
                        nc.scalar.activation(mTr[part][:], bank[0:G * H, 0:P], ACT.Copy).then_inc(done, 1)
                    elif work == "fill" and index[0] == "e1_w1":
                        if index[1]:
                            for b, n in st.drains([("M", "fill", ("e1_w1", index[1] - 1))]):
                                act.wait_ge(drained[b], n)
                        act.wait_ge(full, st.fills(*key))
                        nc.scalar.activation(th, bank[:], ACT.Tanh, scale=0.5).then_inc(silu_tanh, 1)
                    elif work == "fill" and index[0] in HID_AT:
                        if index == ("e0_up", 0):
                            for b, n in st.drains([("M", "fill", ("e1_w1", 1)), ("M", "fill", ("e1_w2", 1))]):
                                act.wait_ge(drained[b], n)
                        act.wait_ge(full, st.fills(*key))
                        nc.scalar.activation(hid[:, HID_AT[index[0]] + index[1], :], bank[:], ACT.Gelu).then_inc(done, 1)
                    elif work == "s2":
                        k = keys[part]
                        act.wait_ge(full, st.fills(*key))
                        nc.scalar.activation(probs[0:k, index[1], :], bank[0:k, :], ACT.Exp,
                                             scale=SCALE if part == "A" else 1.0).then_inc(done, 1)
                    elif work == "pv" and index[1] == NT - 1:
                        act.wait_ge(full, st.fills(*key))
                        nc.scalar.activation(oT, bank[:], ACT.Copy).then_inc(done, 1)
                    elif work == "nT":
                        act.wait_ge(full, st.fills(*key))
                        nc.scalar.activation(onT[:], bank[:, 0:P], ACT.Copy).then_inc(done, 1)

            run_steps(act, step)
            act.wait_ge(stored, NG * 16)

        @block.vector
        def _(dve):
            def statistics(src, stats_of, mv, ve, stats, g):
                for b in range(G):
                    ins = nc.vector.bn_stats(stats_of[:, b, :], src[:, b, :])
                ins.then_inc(stats, 1)
                dve.wait_ge(stats, g * 3 + 1)
                nc.vector.memset(sm[:, 4, 3:4], 0.0)
                for b in range(G):
                    ins = nc.vector.bn_aggr(mv[:, b, :], stats_of[:, b, :])
                ins.then_inc(stats, 1)
                dve.wait_ge(stats, g * 3 + 2)
                nc.vector.tensor_scalar(ve[:], mv[:, :, 1], LN_EPS, None, ALU.add).then_inc(stats, 1)

            def low_part(st, part, to, o, affine, scalar):
                key = (part, {"N": o, "B": o + "T"}[part], 0)
                width = G * keys[to] if o == "k" else TOK
                dve.wait_ge(high_ready[o], uses_of_split(st, part) + 1)
                nc.vector.scalar_tensor_tensor(out=split[o][:, 1, 0:width], in0=psum[BANK[key]][:, 0:width], scalar=scalar,
                                               in1=split[o][:, 0, 0:width].bitcast(F32), op0=affine, op1=ALU.subtract)\
                    .then_inc(drained[BANK[key]], 1)

            def step(st):
                for part, work, index in st.works:
                    key, g = (part, work, index), st.group(part)
                    if key in BANK:
                        bank, full, done = psum[BANK[key]], filled[BANK[key]], drained[BANK[key]]
                    if (part, work) == ("N", "stats"):
                        dve.wait_ge(x_loaded, g * 16 + 16)
                        statistics(xt, stA, mvA, veA, a_stats, g)
                    elif (part, work) == ("N", "norm"):
                        dve.wait_ge(a_rstd, g + 1)
                        for b in range(G):
                            ins = nc.vector.tensor_scalar(xn[:, b, :], xt[:, b, :], mvA[:, b, 0:1], rsA[:, b:b + 1],
                                                          ALU.subtract, ALU.mult)
                        ins.then_inc(xn_ready, 1)
                        if st.parts == "N":
                            nc.vector.memset(qd["A"][:].bitcast(F32), 0.0)
                            nc.vector.memset(kst["A"][:].bitcast(F32), 1.0).then_inc(a_cleared, 1)
                    elif (part, work) == ("A", "stats"):
                        for b, n in st.drains([("A", "wo", b) for b in range(G)]):
                            dve.wait_ge(drained[b], n)
                        statistics(x1, stB, mvB, veB, b_stats, g)
                    elif (part, work) == ("A", "norm"):
                        dve.wait_ge(b_rs, g + 1)
                        for b in range(G):
                            ins = nc.vector.tensor_scalar(hb[:, b, :], x1[:, b, :], mvB[:, b, 0:1], rB[:, 5, b:b + 1],
                                                          ALU.subtract, ALU.mult)
                        ins.then_inc(hb_ready, 1)
                    elif (part, work) == ("B", "norm"):
                        if not st.first("B"):
                            dve.wait_ge(xf_ready, g)
                        for b in range(G):
                            ins = nc.vector.tensor_scalar(x2[:, b, :], x1[:, b, :], mvB[:, b, 0:1], rB[:, 0, b:b + 1],
                                                          ALU.subtract, ALU.mult)
                        ins.then_inc(x2_ready, 1)
                    elif (part, work) == ("M", "squares"):
                        dve.wait_ge(m_sq, g + 1)
                        nc.vector.tensor_reduce(ssM[:], sqM, AX.X, ALU.add).then_inc(m_ms, 1)
                        dve.wait_ge(m_ms, g * 2 + 1)
                        nc.vector.tensor_scalar(msM[:], ssM[:], 1.0 / P, RMS_EPS, ALU.mult, ALU.add).then_inc(m_ms, 1)
                    elif (part, work) in (("N", "q"), ("N", "k")):
                        low_part(st, "N", "A", work, ALU.add, col["b" + work])
                    elif (part, work) in (("B", "qT"), ("B", "kT")):
                        low_part(st, "B", "B", work[0], ALU.mult, qns[:] if work == "qT" else col["kn"])
                    elif (part, work) == ("A", "sums"):
                        dve.wait_ge(sq_ready, g + 1)
                        nc.vector.tensor_reduce(hs[:], sq[:].rearrange("p b (h d) -> p (b h) d", d=HD), AX.X, ALU.add)\
                            .then_inc(hs_ready, 1)
                        dve.wait_ge(hs_ready, g * 2 + 1)
                        nc.vector.tensor_scalar(hs[:], hs[:], 1.0 / HD, RMS_EPS, ALU.mult, ALU.add).then_inc(hs_ready, 1)
                    elif (part, work) == ("A", "scale"):
                        dve.wait_ge(root_ready, g + 1)
                        nc.vector.reciprocal(hr[:], hr[:]).then_inc(hr_ready, 1)
                        dve.wait_ge(hr_ready, g + 1)
                        nc.vector.tensor_tensor(
                            qk[:].rearrange("p b (h d) -> p (b h) d", d=HD), qk[:].rearrange("p b (h d) -> p (b h) d", d=HD),
                            hr[:].rearrange("p (n a) -> p n a", a=1).to_broadcast([P, 2 * H * G, HD]), ALU.mult)\
                            .then_inc(qk_ready, 1)
                    elif (part, work) == ("M", "logits"):
                        logits = bank[:].rearrange("p (b e) -> p b e", b=G)[:, :, 0:E]
                        dve.wait_ge(full, st.fills(*key))
                        nc.vector.tensor_scalar(lg[:, 0], logits, 0.0, F32_MAX, ALU.max, ALU.min)
                        nc.vector.tensor_scalar(lg[:, 1], logits, 0.0, -F32_MAX, ALU.min, ALU.max).then_inc(done, 1)
                    elif (part, work) == ("M", "gates"):
                        choose_experts(st, g, index)
                    elif work == "s1":
                        b, c = index
                        k = keys[part]
                        dve.wait_ge(full, st.fills(*key))
                        nc.vector.tensor_reduce(mneg[part][:, :, c, b],
                                                bank[:, 0:HT * k].rearrange("p (h k) -> p h k", h=HT),
                                                AX.X, ALU.max, negate=True).then_inc(done, 1)
                    elif work == "fill" and index[0] == "e1_w2":
                        c = index[1]
                        u = BANK["M", "fill", ("e1_w1", c)]
                        if c:
                            for b, n in st.drains([("M", "fill", ("e1_w2", c - 1))]):
                                dve.wait_ge(drained[b], n)
                        dve.wait_ge(silu_tanh, g * 2 + c + 1)
                        nc.vector.scalar_tensor_tensor(out=tu, in0=th, scalar=1.0, in1=psum[u][:],
                                                       op0=ALU.add, op1=ALU.mult).then_inc(drained[u], 1)
                        dve.wait_ge(drained[u], st.fills("M", "fill", ("e1_w1", c)))
                        dve.wait_ge(full, st.fills(*key))
                        nc.vector.scalar_tensor_tensor(out=hid[:, HID_AT["e1"] + c, :], in0=tu, scalar=0.5, in1=bank[:],
                                                       op0=ALU.mult, op1=ALU.mult).then_inc(done, 1)
                    elif work == "fill" and index == M_FILLS[-1]:
                        for b, n in st.drains([("M", "fill", [f for f in M_FILLS if f[0] == "down"][-1])]):
                            dve.wait_ge(drained[b], n)
                    elif work == "fill" and index[0] == "down":
                        e = index[1]
                        order = [f for f in M_FILLS if f[0] == "down"] + LATE_FILLS
                        n = order.index(index)
                        if n == 0:
                            dve.wait_ge(y_copied, g + 1)
                        elif index != LATE_FILLS[0]:
                            for b, v in st.drains([(part, "fill", order[n - 1])]):
                                dve.wait_ge(drained[b], v)
                        dve.wait_ge(full, st.fills(*key))
                        for b in range(G):
                            ins = nc.vector.scalar_tensor_tensor(
                                out=ym[:, b, KEEP:P], in0=bank[:, b * UP:(b + 1) * UP], scalar=gates[:, b, e:e + 1],
                                in1=ym[:, b, KEEP:P], op0=ALU.mult, op1=ALU.add)
                        ins.then_inc(done, 1)
                    elif work == "oT":
                        dve.wait_ge(full, st.fills(*key))
                        v = bank[:].rearrange("p (h e) -> p h e", h=H)
                        nc.vector.reciprocal(rden[:].rearrange("p (h a) -> p h a", a=1), v[:, :, HD:VW]).then_inc(rden_ready[part], 1)
                        dve.wait_ge(rden_ready[part], g * G + index + 1)
                        nc.vector.tensor_tensor(on[:].rearrange("p (h d) -> p h d", h=H), v[:, :, 0:HD],
                                                rden[:].rearrange("p (h a) -> p h a", a=1).to_broadcast([P, H, HD]),
                                                ALU.mult).then_inc(done, 1)
                    elif work == "wo" and part == "A":
                        if index == 0:
                            dve.wait_ge(x1_base, g + 1)
                        dve.wait_ge(full, st.fills(*key))
                        nc.vector.scalar_tensor_tensor(out=x1[:, index, :], in0=bank[:, 0:P], scalar=gx, in1=x1[:, index, :],
                                                       op0=ALU.mult, op1=ALU.add).then_inc(done, 1)
                    elif work == "wo":
                        dve.wait_ge(full, st.fills(*key))
                        nc.vector.tensor_tensor(x2[:, index, KEEP:P], bank[:, 0:UP], x2[:, index, KEEP:P],
                                                ALU.add).then_inc(done, 1)
                    elif (part, work) == ("B", "out"):
                        for b, n in st.drains([("B", "wo", b) for b in range(G)]):
                            dve.wait_ge(drained[b], n)
                        dve.wait_ge(x1_copied, g + 1)
                        nc.vector.scalar_tensor_tensor(out=xy[:], in0=x2[:], scalar=gf, in1=xy[:],
                                                       op0=ALU.mult, op1=ALU.add).then_inc(y_ready, 1)

            def choose_experts(st, g, piece):
                n = [(0, 3, 6, 8, 12)[piece]]

                def link(ins):
                    ins.then_inc(gate_step, 1)
                    n[0] += 1
                    dve.wait_ge(gate_step, g * GATE_STEPS + n[0])

                def over_experts(a):
                    return a.rearrange("p (b a) -> p b a", a=1).to_broadcast([P, G, E])

                if piece == 0:
                    spot = BANK["M", "logits", 0]
                    dve.wait_ge(drained[spot], st.fills("M", "logits", 0))
                    link(nc.vector.tensor_tensor(lg[:, 4], lg[:, 0], lg[:, 1], ALU.add))
                    link(nc.vector.tensor_reduce(sm[:, 0], lg[:, 4], AX.X, ALU.max, negate=True))
                    link(nc.vector.tensor_tensor(lg[:, 2], lg[:, 4], over_experts(sm[:, 0]), ALU.add))
                elif piece == 1:
                    dve.wait_ge(gate_exp, g + 1)
                    link(nc.vector.tensor_reduce(sm[:, 1], lg[:, 3], AX.X, ALU.add))
                    link(nc.vector.reciprocal(sm[:, 2], sm[:, 1]))
                    link(nc.vector.tensor_tensor(lg[:, 5], lg[:, 3], over_experts(sm[:, 2]), ALU.mult))
                elif piece == 2:
                    p_j = lg[:, 5].rearrange("p b (a e) -> p b a e", a=1).to_broadcast([P, G, E, E])
                    p_e = lg[:, 5].rearrange("p b (e a) -> p b e a", a=1).to_broadcast([P, G, E, E])
                    for b in range(G):
                        pj, pe_ = p_j[:, b], p_e[:, b]
                        nc.vector.tensor_tensor(cmp[:, 0, b], pj, pe_, ALU.is_gt)
                        last = nc.vector.tensor_tensor(cmp[:, 1, b], pj, pe_, ALU.is_equal)
                    link(last)
                    link(nc.vector.tensor_tensor(cmp[:, 1].rearrange("p b e j -> p b (e j)"), cmp[:, 1].rearrange("p b e j -> p b (e j)"),
                                                 lower[:].rearrange("p (a n) -> p a n", a=1).to_broadcast([P, G, E * E]), ALU.mult))
                elif piece == 3:
                    link(nc.vector.tensor_tensor(cmp[:, 0].rearrange("p b e j -> p (b e j)"), cmp[:, 0].rearrange("p b e j -> p (b e j)"),
                                                 cmp[:, 1].rearrange("p b e j -> p (b e j)"), ALU.add))
                    link(nc.vector.tensor_reduce(lg[:, 6], cmp[:, 0], AX.X, ALU.add))
                    link(nc.vector.tensor_scalar(lg[:, 7], lg[:, 6], 1.5, None, ALU.is_lt))
                    link(nc.vector.tensor_tensor(lg[:, 6], lg[:, 5], lg[:, 7], ALU.mult))
                else:
                    link(nc.vector.tensor_reduce(sm[:, 3], lg[:, 6], AX.X, ALU.add))
                    link(nc.vector.tensor_scalar(sm[:, 1], sm[:, 3], 1e-8, None, ALU.add))
                    link(nc.vector.reciprocal(sm[:, 2], sm[:, 1]))
                    link(nc.vector.scalar_tensor_tensor(out=gates[:], in0=lg[:, 6], scalar=gf, in1=over_experts(sm[:, 2]),
                                                        op0=ALU.mult, op1=ALU.mult))
                    assert n[0] == GATE_STEPS

            nc.vector.memset(kd["A"][:], 0.0)
            for p in "AB":
                nc.vector.memset(mpad[p][:], 0.0)
            nc.vector.memset(psum["pv"][:], 0.0)
            dve.wait_ge(const_loaded, 48)
            dve.wait_ge(setup_act, SETUP_ACT)
            dve.wait_ge(setup_pool, SETUP_POOL)
            dve.wait_ge(setup_pe, 1)
            nc.vector.tensor_tensor(gxbo[:], psum["t"][:, 0:P], bo, ALU.add).then_inc(bias_ready, 1)
            dve.wait_ge(bias_ready, 1)
            nc.vector.tensor_scalar(gxbo[:], gxbo[:], gx, None, ALU.mult).then_inc(bias_ready, 1)
            nc.vector.tensor_scalar(qns[:], col["qn"], SCALE, None, ALU.mult).then_inc(setup_dve, 1)
            dve.wait_ge(setup_dve, 1)
            run_steps(dve, step)

        @block.tensor
        def _(pe):
            mm = nc.tensor.matmul
            pe.wait_ge(const_loaded, 48)
            mm(psum["t"][:, 0:P], col["bv"].to_broadcast([P, P]), w["Wo"], start=True, stop=True).then_inc(setup_pe, 1)
            pe.wait_ge(setup_dve, SETUP_DVE)

            def transposes(st, key, of, n, sources=()):
                for b, v in st.drains(sources, key):
                    pe.wait_ge(drained[b], v)
                for b in range(n):
                    ins = nc.tensor.transpose(psum[BANK[key]][:, b * P:(b + 1) * P], of(b), identf[:])
                ins.then_inc(filled[BANK[key]], 1)

            def step(st):
                for part, work, index in st.works:
                    key, g = (part, work, index), st.group(part)
                    if key in BANK:
                        bank, done = psum[BANK[key]], filled[BANK[key]]
                    if (part, work) == ("N", "xT"):
                        pe.wait_ge(xn_ready, g + 1)
                        transposes(st, key, lambda b: xn[:, b, :], G)
                    elif (part, work) == ("N", "q"):
                        for b, v in st.drains([("N", "xT", 0)], key):
                            pe.wait_ge(drained[b], v)
                        mm(bank[:], w["Wq"], xnT[:], start=True, stop=True).then_inc(done, 1)
                    elif (part, work) == ("N", "k"):
                        pe.wait_ge(ctx_loaded, g * 16 + 16)
                        for b, v in st.drains([], key):
                            pe.wait_ge(drained[b], v)
                        mm(bank[:, 0:CT], w["Wk"][0:DC, :], ctT[:], start=True, stop=True).then_inc(done, 1)
                    elif (part, work) == ("N", "v"):
                        for b, v in st.drains([], key):
                            pe.wait_ge(drained[b], v)
                        for b in range(G):
                            ins = mm(bank[0:KV, b * P:(b + 1) * P], ctT[:, b * KV:(b + 1) * KV], w["Wv"][0:DC, :],
                                     start=True, stop=True)
                        ins.then_inc(done, 1)
                    elif (part, work) == ("M", "xfT"):
                        pe.wait_ge(xf_ready, g + 1)
                        transposes(st, key, lambda b: xf[:, b, :], G)
                    elif (part, work) == ("M", "logits"):
                        for b, v in st.drains([("M", "xfT", 0)], key):
                            pe.wait_ge(drained[b], v)
                        for b in range(G):
                            ins = mm(bank[:, b * P:(b + 1) * P], xfT[:, b * P:(b + 1) * P], w["gate"], start=True, stop=True)
                        ins.then_inc(done, 1)
                    elif (part, work) == ("A", "hT"):
                        pe.wait_ge(hb_ready, g + 1)
                        transposes(st, key, lambda b: hb[:, b, :], G)
                    elif (part, work) == ("A", "qk"):
                        for b, v in st.drains([("A", "hT", 0)], key):
                            pe.wait_ge(drained[b], v)
                        mm(bank[:, 0:2 * P], hT[:, index * P:(index + 1) * P], w["wqk"], start=True, stop=True).then_inc(done, 1)
                    elif (part, work) == ("B", "v"):
                        for b, v in st.drains([], key):
                            pe.wait_ge(drained[b], v)
                        for b in range(G):
                            ins = mm(bank[:, b * P:(b + 1) * P], hT[:, b * P:(b + 1) * P], w["wv"], start=True, stop=True)
                        ins.then_inc(done, 1)
                    elif (part, work) in (("B", "qT"), ("B", "kT")):
                        pe.wait_ge(qk_ready, g + 1)
                        first = 0 if work == "qT" else P
                        transposes(st, key, lambda b: qk[:, b, first:first + P], G)
                    elif work == "s1":
                        b, c = index
                        k = keys[part]
                        if index == (0, 0):
                            pe.wait_ge(cast_ready[part], g * 2 + 2)
                            pe.wait_ge(kd_loaded[part], g * GROUP_KD + GROUP_KD)
                        for bk, v in st.drains([], key):
                            pe.wait_ge(drained[bk], v)
                        o = bank[:, 0:HT * k].rearrange("p (h k) -> p h k", h=HT)
                        ins = mm(o, qTb[part][:, b * P:(b + 1) * P], kd[part][:, c * HT:(c + 1) * HT, b * k:(b + 1) * k],
                                 start=True, stop=part == "A")
                        if part == "B":
                            ins = mm(o, identb[:], above[:].to_broadcast([P, HT, P]), start=False, stop=True)
                        ins.then_inc(done, 1)
                    elif work == "mT":
                        for b, v in st.drains([(part, "s1", (G - 1, NT - 1)), (part, "s1", (G - 1, NT - 2))], key):
                            pe.wait_ge(drained[b], v)
                        nc.tensor.transpose(bank[:, 0:P], mpad[part][:], identf[:]).then_inc(done, 1)
                    elif work == "s2":
                        b, c = index
                        k = keys[part]
                        if index == (0, 0):
                            pe.wait_ge(stacks_loaded[part], g * GROUP_STACKS + GROUP_STACKS)
                            pe.wait_ge(m_loaded[part], g * GROUP_M + GROUP_M)
                        for bk, v in st.drains([], key):
                            pe.wait_ge(drained[bk], v)
                        o = bank[0:k, :].rearrange("p (h q) -> p h q", h=HT)
                        ins = mm(o, kst[part][:, c, b * k:(b + 1) * k], qd[part][:, :, c, b * P:(b + 1) * P],
                                 start=True, stop=part == "A")
                        if part == "B":
                            ins = mm(o, above[:, 0, :], identb[:].rearrange("p (a q) -> p a q", a=1).to_broadcast([P, HT, P]),
                                     start=False, stop=True)
                        ins.then_inc(done, 1)
                    elif work == "pv":
                        b, c = index
                        k = keys[part]
                        last = (part, "pv", (b, NT - 1))
                        sources = [(part, "s2", index)] + ([("B", "v", 0)] if part == "B" and index == (0, 0) else [])
                        for bk, v in st.drains(sources, last if c == 0 else None):
                            pe.wait_ge(drained[bk], v)
                        for j in range(HT):
                            ins = mm(psum[BANK[last]][32 * j:32 * j + VW, c * P:(c + 1) * P], V[part][0:k, b, c * HT + j, :],
                                     probs[0:k, c, j * P:(j + 1) * P], start=True, stop=True)
                        if c == NT - 1:
                            ins.then_inc(filled[BANK[last]], 1)
                    elif work == "oT":
                        transposes(st, key, lambda c: oT[:, c * P:(c + 1) * P], NT, [(part, "pv", (index, NT - 1))])
                    elif work == "nT":
                        transposes(st, key, lambda c: on[:], 1, [(part, "oT", index)])
                    elif work == "wo":
                        for b, v in st.drains([(part, "nT", index)], key):
                            pe.wait_ge(drained[b], v)
                        n = P if part == "A" else UP
                        mm(bank[:, 0:n], onT[:], w["Wo"] if part == "A" else w["wo"], start=True, stop=True).then_inc(done, 1)
                    elif work == "fill" and index[0] == "down":
                        h = DOWN_OF[index[1]]
                        sources = [(part, "fill", ("e1_w2" if h == "e1" else h, k)) for k in range(2) if part == "M"]
                        for b, v in st.drains(sources, key):
                            pe.wait_ge(drained[b], v)
                        for b in range(G):
                            for k in range(2):
                                ins = mm(bank[:, b * UP:(b + 1) * UP], hid[:, HID_AT[h] + k, b * P:(b + 1) * P],
                                         w[f"down{index[1]}"][:, k * UP:(k + 1) * UP], start=k == 0, stop=k == 1)
                        ins.then_inc(done, 1)
                    elif work == "fill" and index[0] in ("e2_l2", "e2_l3", "e3_up"):
                        name, c = index
                        h = {"e2_l2": "e2_l1", "e2_l3": "e2_l2", "e3_up": "e3_down"}[name]
                        chunks = range(1 if name == "e3_up" else 2)
                        for b, v in st.drains([("M", "fill", (h, k)) for k in chunks], key):
                            pe.wait_ge(drained[b], v)
                        for k in chunks:
                            ins = mm(bank[:], w[name][:, k * HID + c * P:k * HID + (c + 1) * P], hid[:, HID_AT[h] + k, :],
                                     start=k == 0, stop=k == chunks[-1])
                        ins.then_inc(done, 1)
                    elif work == "fill":
                        name, c = index
                        for b, v in st.drains([("M", "xfT", 0)], key):
                            pe.wait_ge(drained[b], v)
                        mm(bank[:], w[name][:, c * P:(c + 1) * P], xfT[:], start=True, stop=True).then_inc(done, 1)

            run_steps(pe, step)


def kernel(**inputs):
    import numpy as _np
    import concourse.bacc as _bacc
    from concourse.bass_utils import run_bass_kernel_spmd as _run

    i = {k: _np.asarray(v) for k, v in inputs.items()}
    f = {k.replace("L0_ffn_", ""): v for k, v in i.items() if k.startswith("L0_ffn_")}
    a = {k.replace("L0_xattn_", ""): v for k, v in i.items() if k.startswith("L0_xattn_")}

    def wide(m):
        out = _np.zeros((P, m.shape[1]), m.dtype)
        out[:m.shape[0]] = m
        return out

    def chunks(m):
        return _np.concatenate([m[:P], m[P:]], axis=1)

    parts = {"Wq": a["Wq"], "Wk": wide(a["Wk"]), "Wv": wide(a["Wv"]), "Wo": a["Wo"],
             "wqk": _np.concatenate([f["wq"].T, f["wk"].T], axis=1), "wv": f["wv"].T, "wo": f["wo"].T[:, KEEP:],
             "gate": wide(f["gate_w"]).T, "e0_up": f["e0_up"].T, "e1_w1": f["e1_w1"].T, "e1_w2": f["e1_w2"].T,
             "e2_l1": f["e2_l1"].T, "e2_l2": chunks(f["e2_l2"].T), "e2_l3": chunks(f["e2_l3"].T),
             "e3_down": f["e3_down"].T, "e3_up": f["e3_up"].T,
             "down0": chunks(f["e0_down"].T[:, KEEP:]), "down1": chunks(f["e1_down"].T[:, KEEP:]),
             "down2": chunks(f["e2_l4"].T[:, KEEP:]), "down3": chunks(f["e3_out"].T[:, KEEP:])}
    cols = {"bv": a["bv"], "bq": a["bq"], "bk": a["bk"], "n1": f["n1_w"], "n2": f["n2_w"], "qn": _np.tile(f["qn_w"], H),
            "kn": _np.tile(f["kn_w"], H), "gx": _np.repeat(i["g_xattn"], P), "gf": _np.repeat(i["g_ffn"], P)}
    arrays = {
        "x": _np.ascontiguousarray(i["x"]),
        "ctxT": _np.ascontiguousarray(i["ctx_768"].reshape(SEQS * KV, DC).T),
        "weights": _np.ascontiguousarray(_np.concatenate([parts[n] for n, _ in WCOLS], axis=1)),
        "vcols": _np.ascontiguousarray(_np.stack([cols[n] for n in VCOLS], axis=1)),
        "rows": _np.ascontiguousarray(_np.broadcast_to(_np.concatenate([a[n] for n in ROWS]), (P, len(ROWS) * P))),
    }
    nc = _bacc.Bacc("TRN2", target_bir_lowering=False, num_devices=1)
    args = [nc.dram_tensor(f"in_{n}", v.shape, mybir.dt.from_np(v.dtype), kind="ExternalInput").ap() for n, v in arrays.items()]
    o = nc.dram_tensor("out_x", (SEQS, P, P), F32, kind="ExternalOutput").ap()
    build(nc, *args, o)
    r = _run(nc, [{f"in_{n}": v for n, v in arrays.items()}], core_ids=[0])
    return r.results[0]["out_x"]
```
